# Optimizing a Trainium2 kernel written in Bass

```python
import numpy as np
import jax
import jax.numpy as jnp

def _softmax(x, axis=-1):
    return jax.nn.softmax(x, axis=axis)

def _gelu(x):
    return jax.nn.gelu(x, approximate=True)

def _silu(x):
    return jax.nn.silu(x)

def _sigmoid(x):
    return jax.nn.sigmoid(x)

def _layernorm(x, axis=-1, eps=1e-05):
    m = jnp.mean(x, axis=axis, keepdims=True)
    v = jnp.var(x, axis=axis, keepdims=True)
    return (x - m) / jnp.sqrt(v + eps)

def _scatter_add(tgt, idx, src, axis=0):
    return tgt.at[idx].add(src)

def _segment_sum(src, seg, n):
    return jax.ops.segment_sum(src, seg, n)
kernel_name = 'mk_hybrid_d2_jaxref_r8_6c3814'

def setup_inputs(seed: int=0):
    np.random.seed(seed)
    _w = jnp.asarray

    def _L0_attn_a_setup():
        import jax, jax.numpy as jnp
        import numpy as np
        DIMS = 256
        HEAD = 16
        HD = DIMS // HEAD
        EPS = float(np.finfo(np.float32).eps)

        def _rms(x, g):
            return x * jax.lax.rsqrt(jnp.mean(x * x, axis=-1, keepdims=True) + EPS) * g
        key = jax.random.key(seed)
        ks = jax.random.split(key, 8)
        B, T, D = (2, 256, DIMS)
        s = 1.0 / np.sqrt(D)
        return {'x': jax.random.normal(ks[0], (B, T, D), dtype=jnp.float32), 'g_q': jnp.ones((D,), jnp.float32), 'Wq': jax.random.normal(ks[1], (D, D), jnp.float32) * s, 'bq': jnp.zeros((D,), jnp.float32), 'g_kv': jnp.ones((D,), jnp.float32), 'Wkv': jax.random.normal(ks[2], (D, 2 * D), jnp.float32) * s, 'bkv': jnp.zeros((2 * D,), jnp.float32), 'g_head': jnp.ones((HD,), jnp.float32), 'Wo': jax.random.normal(ks[3], (D, D), jnp.float32) * s, 'bo': jnp.zeros((D,), jnp.float32)}
    _L0_attn_a_in = _L0_attn_a_setup()

    def _L0_attn_b_setup():
        import jax, jax.numpy as jnp
        import numpy as np
        B, S, H = (4, 256, 256)
        key = jax.random.key(seed)
        k1, k2, k3 = jax.random.split(key, 3)
        xav_qkv = float(np.sqrt(6.0 / (H + 3 * H)))
        xav_out = float(np.sqrt(6.0 / (H + H)))
        return {'hidden_states': jax.random.normal(k1, (B, S, H), dtype=jnp.float32), 'w_qkv': jax.random.uniform(k2, (3 * H, H), minval=-xav_qkv, maxval=xav_qkv, dtype=jnp.float32), 'b_qkv': jnp.zeros((3 * H,), dtype=jnp.float32), 'w_out': jax.random.uniform(k3, (H, H), minval=-xav_out, maxval=xav_out, dtype=jnp.float32), 'b_out': jnp.zeros((H,), dtype=jnp.float32)}
    _L0_attn_b_in = _L0_attn_b_setup()

    def _L0_ffn_setup():
        import jax, jax.numpy as jnp
        import numpy as np
        from jax import lax
        TOP_K = 2
        N_EXPERTS = 8
        key = jax.random.key(seed)
        ks = jax.random.split(key, 7)
        B, S, H, I, E = (4, 256, 256, 176, N_EXPERTS)
        s_h = 1.0 / np.sqrt(H)
        s_i = 1.0 / np.sqrt(I)
        return {'hidden_states': jax.random.normal(ks[0], (B, S, H), jnp.float32), 'gate_w': jax.random.normal(ks[1], (E, H), jnp.float32) * s_h, 'w1': jax.random.normal(ks[2], (E, H, 2 * I), jnp.float32) * s_h, 'w2': jax.random.normal(ks[3], (E, I, H), jnp.float32) * s_i, 'sw1': jax.random.normal(ks[4], (I, H), jnp.float32) * s_h, 'sw2': jax.random.normal(ks[5], (I, H), jnp.float32) * s_h, 'sw3': jax.random.normal(ks[6], (H, I), jnp.float32) * s_i}
    _L0_ffn_in = _L0_ffn_setup()

    def _L1_attn_a_setup():
        import jax, jax.numpy as jnp
        import numpy as np
        D_MODEL = 256
        N_HEADS = 16
        D_HEAD = D_MODEL // N_HEADS
        B, S = (2, 256)
        EPS = 1e-05

        def _mhsa(X, ln_g, ln_b, Wq, bq, Wk, bk, Wv, bv, Wo, bo):
            n_ctx = X.shape[-2]
            mu = jnp.mean(X, axis=-1, keepdims=True)
            var = jnp.mean(jnp.square(X - mu), axis=-1, keepdims=True)
            Xn = (X - mu) * jax.lax.rsqrt(var + EPS) * ln_g + ln_b

            def split_heads(t):
                return t.reshape(t.shape[:-1] + (N_HEADS, D_HEAD)).swapaxes(-2, -3)
            Q = split_heads(Xn @ Wq + bq)
            K = split_heads(Xn @ Wk + bk)
            V = split_heads(Xn @ Wv + bv)
            scores = jnp.einsum('bhqd,bhkd->bhqk', Q, K) / jnp.sqrt(jnp.float32(D_HEAD))
            causal = jnp.tril(jnp.ones((n_ctx, n_ctx), dtype=bool))
            scores = jnp.where(causal, scores, jnp.float32(-jnp.inf))
            A = jax.nn.softmax(scores, axis=-1)
            AV = jnp.einsum('bhqk,bhkd->bhqd', A, V)
            AV = AV.swapaxes(-2, -3).reshape(X.shape[:-1] + (D_MODEL,))
            return AV @ Wo + bo
        key = jax.random.key(seed)
        ks = jax.random.split(key, 10)
        sd = 1.0 / np.sqrt(D_MODEL)
        inp = {'X': jax.random.normal(ks[0], (B, S, D_MODEL), dtype=jnp.float32), 'ln_g': jnp.ones((D_MODEL,), jnp.float32), 'ln_b': jnp.zeros((D_MODEL,), jnp.float32), 'Wq': jax.random.uniform(ks[1], (D_MODEL, D_MODEL), jnp.float32, -sd, sd), 'bq': jax.random.uniform(ks[2], (D_MODEL,), jnp.float32, -sd, sd), 'Wk': jax.random.uniform(ks[3], (D_MODEL, D_MODEL), jnp.float32, -sd, sd), 'bk': jax.random.uniform(ks[4], (D_MODEL,), jnp.float32, -sd, sd), 'Wv': jax.random.uniform(ks[5], (D_MODEL, D_MODEL), jnp.float32, -sd, sd), 'bv': jax.random.uniform(ks[6], (D_MODEL,), jnp.float32, -sd, sd), 'Wo': jax.random.uniform(ks[7], (D_MODEL, D_MODEL), jnp.float32, -sd, sd), 'bo': jax.random.uniform(ks[8], (D_MODEL,), jnp.float32, -sd, sd)}
        return inp
    _L1_attn_a_in = _L1_attn_a_setup()

    def _L1_attn_b_setup():
        import jax, jax.numpy as jnp
        import numpy as np
        import math
        HQ, HKV = (32, 8)
        key = jax.random.key(seed)
        ks = jax.random.split(key, 5)
        B, S, D = (2, 256, 256)
        hd = D // HQ
        w = lambda k, i, o: jax.random.normal(k, (i, o), jnp.float32) / math.sqrt(i)
        return {'x': jax.random.normal(ks[0], (B, S, D), jnp.float32), 'Wq': w(ks[1], D, D), 'Wk': w(ks[2], D, HKV * hd), 'Wv': w(ks[3], D, HKV * hd), 'Wo': w(ks[4], D, D)}
    _L1_attn_b_in = _L1_attn_b_setup()

    def _L1_ffn_setup():
        import jax, jax.numpy as jnp
        import numpy as np
        B, S, D, H = (4, 256, 256, 1024)

        def fwht(x):
            orig_shape = x.shape
            n = orig_shape[-1]
            x = x.reshape(-1, n)
            h = 1
            while h < n:
                xb = x.reshape(-1, n // (2 * h), 2, h)
                a = xb[:, :, 0, :]
                b = xb[:, :, 1, :]
                x = jnp.stack([a + b, a - b], axis=2).reshape(-1, n)
                h *= 2
            scale = jnp.asarray(1.0 / np.sqrt(n), dtype=x.dtype)
            return (x * scale).reshape(orig_shape)
        key = jax.random.key(seed)
        kx, k1, k2, k3 = jax.random.split(key, 4)
        x = jax.random.normal(kx, (B, S, D), dtype=jnp.float32)
        W1 = jax.random.normal(k1, (H, D), dtype=jnp.float32) * (1.0 / np.sqrt(D))
        W2 = jax.random.normal(k2, (D, H), dtype=jnp.float32) * (1.0 / np.sqrt(H))
        W3 = jax.random.normal(k3, (H, D), dtype=jnp.float32) * (1.0 / np.sqrt(D))
        return {'x': x, 'W1': W1, 'W2': W2, 'W3': W3}
    _L1_ffn_in = _L1_ffn_setup()
    _d = {'L0_attn_a_x': _L0_attn_a_in['x'], 'L0_attn_a_g_q': _L0_attn_a_in['g_q'], 'L0_attn_a_Wq': _L0_attn_a_in['Wq'], 'L0_attn_a_bq': _L0_attn_a_in['bq'], 'L0_attn_a_g_kv': _L0_attn_a_in['g_kv'], 'L0_attn_a_Wkv': _L0_attn_a_in['Wkv'], 'L0_attn_a_bkv': _L0_attn_a_in['bkv'], 'L0_attn_a_g_head': _L0_attn_a_in['g_head'], 'L0_attn_a_Wo': _L0_attn_a_in['Wo'], 'L0_attn_a_bo': _L0_attn_a_in['bo'], 'L0_attn_b_w_qkv': _L0_attn_b_in['w_qkv'], 'L0_attn_b_b_qkv': _L0_attn_b_in['b_qkv'], 'L0_attn_b_w_out': _L0_attn_b_in['w_out'], 'L0_attn_b_b_out': _L0_attn_b_in['b_out'], 'L0_ffn_gate_w': _L0_ffn_in['gate_w'], 'L0_ffn_w1': _L0_ffn_in['w1'], 'L0_ffn_w2': _L0_ffn_in['w2'], 'L0_ffn_sw1': _L0_ffn_in['sw1'], 'L0_ffn_sw2': _L0_ffn_in['sw2'], 'L0_ffn_sw3': _L0_ffn_in['sw3'], 'L1_attn_a_ln_g': _L1_attn_a_in['ln_g'], 'L1_attn_a_ln_b': _L1_attn_a_in['ln_b'], 'L1_attn_a_Wq': _L1_attn_a_in['Wq'], 'L1_attn_a_bq': _L1_attn_a_in['bq'], 'L1_attn_a_Wk': _L1_attn_a_in['Wk'], 'L1_attn_a_bk': _L1_attn_a_in['bk'], 'L1_attn_a_Wv': _L1_attn_a_in['Wv'], 'L1_attn_a_bv': _L1_attn_a_in['bv'], 'L1_attn_a_Wo': _L1_attn_a_in['Wo'], 'L1_attn_a_bo': _L1_attn_a_in['bo'], 'L1_attn_b_Wq': _L1_attn_b_in['Wq'], 'L1_attn_b_Wk': _L1_attn_b_in['Wk'], 'L1_attn_b_Wv': _L1_attn_b_in['Wv'], 'L1_attn_b_Wo': _L1_attn_b_in['Wo'], 'L1_ffn_W1': _L1_ffn_in['W1'], 'L1_ffn_W2': _L1_ffn_in['W2'], 'L1_ffn_W3': _L1_ffn_in['W3']}
    _x0 = _d['L0_attn_a_x']
    _d['L0_attn_a_x'] = jax.random.normal(jax.random.fold_in(jax.random.key(seed), 1), (2, 1024, 256), dtype=_x0.dtype)
    del _x0
    return _d

def reference(L0_attn_a_x, L0_attn_a_g_q, L0_attn_a_Wq, L0_attn_a_bq, L0_attn_a_g_kv, L0_attn_a_Wkv, L0_attn_a_bkv, L0_attn_a_g_head, L0_attn_a_Wo, L0_attn_a_bo, L0_attn_b_w_qkv, L0_attn_b_b_qkv, L0_attn_b_w_out, L0_attn_b_b_out, L0_ffn_gate_w, L0_ffn_w1, L0_ffn_w2, L0_ffn_sw1, L0_ffn_sw2, L0_ffn_sw3, L1_attn_a_ln_g, L1_attn_a_ln_b, L1_attn_a_Wq, L1_attn_a_bq, L1_attn_a_Wk, L1_attn_a_bk, L1_attn_a_Wv, L1_attn_a_bv, L1_attn_a_Wo, L1_attn_a_bo, L1_attn_b_Wq, L1_attn_b_Wk, L1_attn_b_Wv, L1_attn_b_Wo, L1_ffn_W1, L1_ffn_W2, L1_ffn_W3):

    def _L0_attn_a_ref(x, g_q, Wq, bq, g_kv, Wkv, bkv, g_head, Wo, bo):
        import jax, jax.numpy as jnp
        import numpy as np
        DIMS = 256
        HEAD = 16
        HD = DIMS // HEAD
        EPS = float(np.finfo(np.float32).eps)

        def _rms(x, g):
            return x * jax.lax.rsqrt(jnp.mean(x * x, axis=-1, keepdims=True) + EPS) * g
        B, T, D = x.shape
        H, d = (HEAD, HD)
        q = (_rms(x, g_q) @ Wq + bq).reshape(B, T, H, d).transpose(0, 2, 1, 3)
        kv = (_rms(x, g_kv) @ Wkv + bkv).reshape(B, T, 2, H, d)
        k = kv[:, :, 0].transpose(0, 2, 1, 3)
        v = kv[:, :, 1].transpose(0, 2, 1, 3)
        scale = d ** (-0.5)
        scores = jnp.einsum('bhqd,bhkd->bhqk', _rms(q, g_head), _rms(k, g_head)) * scale
        attn = jax.nn.softmax(scores, axis=-1)
        wv = jnp.einsum('bhqk,bhkd->bhqd', attn, v)
        out = wv.transpose(0, 2, 1, 3).reshape(B, T, D) @ Wo + bo
        return out

    def _L0_attn_b_ref(hidden_states, w_qkv, b_qkv, w_out, b_out):
        import jax, jax.numpy as jnp
        import numpy as np
        B, S, H = (4, 256, 256)
        Bc, Sc, Hc = hidden_states.shape
        scaling = jnp.sqrt(jnp.asarray(Hc, hidden_states.dtype))
        qkv = jnp.einsum('bsh,oh->bso', hidden_states, w_qkv) + b_qkv
        q, k, v = jnp.split(qkv, 3, axis=-1)
        scores = jnp.einsum('bqh,bkh->bqk', q, k) / scaling
        probs = jax.nn.softmax(scores, axis=-1)
        context = jnp.einsum('bqk,bkh->bqh', probs, v)
        out = jnp.einsum('bsh,oh->bso', context, w_out) + b_out
        return out

    def _L0_ffn_ref(hidden_states, gate_w, w1, w2, sw1, sw2, sw3):
        import jax, jax.numpy as jnp
        import numpy as np
        from jax import lax
        TOP_K = 2
        N_EXPERTS = 8
        B, S, H = hidden_states.shape
        x = hidden_states.reshape(-1, H)
        T = x.shape[0]
        logits = jnp.einsum('th,eh->te', x.astype(jnp.float32), gate_w.astype(jnp.float32))
        scores = jax.nn.softmax(logits, axis=-1)
        topk_w, topk_idx = lax.top_k(scores, TOP_K)
        topk_w = topk_w / (topk_w.sum(-1, keepdims=True) + 1e-20)
        topk_w = topk_w.astype(hidden_states.dtype)
        cw = jnp.zeros((T, N_EXPERTS), hidden_states.dtype).at[jnp.arange(T)[:, None], topk_idx].add(topk_w)

        def body(acc, ew):
            w1e, w2e, cwe = ew
            h = x @ w1e
            g, u = jnp.split(h, 2, axis=-1)
            y = jax.nn.silu(g) * u @ w2e
            return (acc + cwe[:, None] * y, None)
        moe, _ = lax.scan(body, jnp.zeros_like(x), (w1, w2, cw.T))
        moe = moe.reshape(B, S, H)
        shared = jnp.einsum('bsi,hi->bsh', jax.nn.silu(jnp.einsum('bsh,ih->bsi', hidden_states, sw1)) * jnp.einsum('bsh,ih->bsi', hidden_states, sw2), sw3)
        return moe + shared

    def _L1_attn_a_ref(X, ln_g, ln_b, Wq, bq, Wk, bk, Wv, bv, Wo, bo):
        import jax, jax.numpy as jnp
        import numpy as np
        D_MODEL = 256
        N_HEADS = 16
        D_HEAD = D_MODEL // N_HEADS
        B, S = (2, 256)
        EPS = 1e-05

        def _mhsa(X, ln_g, ln_b, Wq, bq, Wk, bk, Wv, bv, Wo, bo):
            n_ctx = X.shape[-2]
            mu = jnp.mean(X, axis=-1, keepdims=True)
            var = jnp.mean(jnp.square(X - mu), axis=-1, keepdims=True)
            Xn = (X - mu) * jax.lax.rsqrt(var + EPS) * ln_g + ln_b

            def split_heads(t):
                return t.reshape(t.shape[:-1] + (N_HEADS, D_HEAD)).swapaxes(-2, -3)
            Q = split_heads(Xn @ Wq + bq)
            K = split_heads(Xn @ Wk + bk)
            V = split_heads(Xn @ Wv + bv)
            scores = jnp.einsum('bhqd,bhkd->bhqk', Q, K) / jnp.sqrt(jnp.float32(D_HEAD))
            causal = jnp.tril(jnp.ones((n_ctx, n_ctx), dtype=bool))
            scores = jnp.where(causal, scores, jnp.float32(-jnp.inf))
            A = jax.nn.softmax(scores, axis=-1)
            AV = jnp.einsum('bhqk,bhkd->bhqd', A, V)
            AV = AV.swapaxes(-2, -3).reshape(X.shape[:-1] + (D_MODEL,))
            return AV @ Wo + bo
        return _mhsa(X, ln_g, ln_b, Wq, bq, Wk, bk, Wv, bv, Wo, bo)

    def _L1_attn_b_ref(x, Wq, Wk, Wv, Wo):
        import jax, jax.numpy as jnp
        import numpy as np
        import math
        HQ, HKV = (32, 8)
        B, S, D = x.shape
        hd = D // HQ
        G = HQ // HKV
        scale = 1.0 / math.sqrt(hd)
        q = (x @ Wq).reshape(B, S, HKV, G, hd)
        k = (x @ Wk).reshape(B, S, HKV, hd)
        v = (x @ Wv).reshape(B, S, HKV, hd)
        scores = jnp.einsum('bskgd,btkd->bkgst', q, k) * scale
        causal = jnp.tril(jnp.ones((S, S), dtype=bool))
        scores = jnp.where(causal, scores, jnp.float32(-jnp.inf))
        probs = jax.nn.softmax(scores, axis=-1)
        o = jnp.einsum('bkgst,btkd->bskgd', probs, v)
        o = o.reshape(B, S, D)
        return o @ Wo

    def _L1_ffn_ref(x, W1, W2, W3):
        import jax, jax.numpy as jnp
        import numpy as np
        B, S, D, H = (4, 256, 256, 1024)

        def fwht(x):
            orig_shape = x.shape
            n = orig_shape[-1]
            x = x.reshape(-1, n)
            h = 1
            while h < n:
                xb = x.reshape(-1, n // (2 * h), 2, h)
                a = xb[:, :, 0, :]
                b = xb[:, :, 1, :]
                x = jnp.stack([a + b, a - b], axis=2).reshape(-1, n)
                h *= 2
            scale = jnp.asarray(1.0 / np.sqrt(n), dtype=x.dtype)
            return (x * scale).reshape(orig_shape)
        up_gate = jnp.einsum('bsd,hd->bsh', x, W1)
        up_lin = jnp.einsum('bsd,hd->bsh', x, W3)
        hidden = jax.nn.silu(up_gate) * up_lin
        hidden = fwht(hidden)
        out = jnp.einsum('bsh,dh->bsd', hidden, W2)
        return out
    x = L0_attn_a_x
    x = x + _L0_attn_a_ref(_layernorm(x, axis=-1), L0_attn_a_g_q, L0_attn_a_Wq, L0_attn_a_bq, L0_attn_a_g_kv, L0_attn_a_Wkv, L0_attn_a_bkv, L0_attn_a_g_head, L0_attn_a_Wo, L0_attn_a_bo)
    x = x + _L0_ffn_ref(_layernorm(x, axis=-1), L0_ffn_gate_w, L0_ffn_w1, L0_ffn_w2, L0_ffn_sw1, L0_ffn_sw2, L0_ffn_sw3)
    x = x + _L0_attn_b_ref(_layernorm(x, axis=-1), L0_attn_b_w_qkv, L0_attn_b_b_qkv, L0_attn_b_w_out, L0_attn_b_b_out)
    x = x + _L0_ffn_ref(_layernorm(x, axis=-1), L0_ffn_gate_w, L0_ffn_w1, L0_ffn_w2, L0_ffn_sw1, L0_ffn_sw2, L0_ffn_sw3)
    x = x + _L1_attn_a_ref(_layernorm(x, axis=-1), L1_attn_a_ln_g, L1_attn_a_ln_b, L1_attn_a_Wq, L1_attn_a_bq, L1_attn_a_Wk, L1_attn_a_bk, L1_attn_a_Wv, L1_attn_a_bv, L1_attn_a_Wo, L1_attn_a_bo)
    x = x + _L1_ffn_ref(_layernorm(x, axis=-1), L1_ffn_W1, L1_ffn_W2, L1_ffn_W3)
    x = x + _L1_attn_b_ref(_layernorm(x, axis=-1), L1_attn_b_Wq, L1_attn_b_Wk, L1_attn_b_Wv, L1_attn_b_Wo)
    x = x + _L1_ffn_ref(_layernorm(x, axis=-1), L1_ffn_W1, L1_ffn_W2, L1_ffn_W3)
    return x

_drawn_inputs = setup_inputs


def setup_inputs(seed=0):
    import zlib

    import numpy as np

    out = dict(_drawn_inputs(seed))
    spreads = {'L0_attn_a_g_q': (1.0, 0.2),
     'L0_attn_a_bq': (0.0, 0.1),
     'L0_attn_a_g_kv': (1.0, 0.2),
     'L0_attn_a_bkv': (0.0, 0.1),
     'L0_attn_a_g_head': (1.0, 0.2),
     'L0_attn_a_bo': (0.0, 0.1),
     'L0_attn_b_b_qkv': (0.0, 0.1),
     'L0_attn_b_b_out': (0.0, 0.1),
     'L1_attn_a_ln_g': (1.0, 0.6),
     'L1_attn_a_ln_b': (0.0, 0.299)}
    factors = {'L1_attn_a_Wq': 6.199,
     'L1_attn_a_bq': 8.0,
     'L1_attn_a_Wk': 6.252,
     'L1_attn_a_bk': 8.0,
     'L1_attn_a_bv': 3.452}
    for name, (base, spread) in spreads.items():
        noise = np.random.default_rng([zlib.crc32(name.encode()), seed]).standard_normal(out[name].shape)
        drawn = base * np.exp(spread * noise) if base else spread * noise
        out[name] = jnp.asarray(drawn.astype(out[name].dtype))
    for name, factor in factors.items():
        out[name] = (out[name] * factor).astype(out[name].dtype)
    return out
```

```python
from contextlib import ExitStack

import concourse.bass as bass
from concourse import mybir

F32 = mybir.dt.float32
F32R = mybir.dt.float32r
BF16 = mybir.dt.bfloat16
ACT = mybir.ActivationFunctionType
ALU = mybir.AluOpType
AX = mybir.AxisListType

P = 128
D = 256
KT = D // P
B, S = 2, 1024
T = B * S
NT = T // P
CH = 512
NCH = T // CH
TPC = CH // P
ST = S // P
ROWS = 96
NEG = -1e30
LN_EPS = 1e-5
RMS_EPS = 1.1920928955078125e-07


class Phase:

    def __init__(self, nc, name):
        self.nc, self.name, self.stack, self.sems = nc, name, ExitStack(), []

    def __enter__(self):
        self.stack.__enter__()
        return self

    def sb(self, name, shape, dt=F32):
        return self.stack.enter_context(self.nc.sbuf_tensor(f"{self.name}_{name}", shape, dt))

    def psum(self, name, shape, dt=F32):
        return self.stack.enter_context(self.nc.psum_tensor(f"{self.name}_{name}", shape, dt))

    def sem(self, name):
        s = self.nc.alloc_semaphore(f"{self.name}_{name}")
        self.sems.append(s)
        return s

    def __exit__(self, *exc):
        if exc[0] is None:
            self.nc.clear_and_free_semaphores(self.sems)
            self.nc.all_engine_barrier()
        return self.stack.__exit__(*exc)


CREDIT = 2


def nth(n):
    return n + 1


def cnth(n):
    return n + (1 + CREDIT)


def two_back(n):
    return n + (CREDIT - 1)


def f(ap):
    return ap.bitcast(F32)


def three_terms(pe, out, pairs, start=True, stop=True):
    last = None
    for n, ((ah, al), (bh, bl)) in enumerate(pairs):
        for m, (a, b) in enumerate(((ah, bh), (al, bh), (ah, bl))):
            last = pe.matmul(out, a, b, start=start and n == 0 and m == 0,
                             stop=stop and n == len(pairs) - 1 and m == 2)
    return last


def setup(nc, x, X, ident, ident_bf, mask_qk, mask_kq):
    with Phase(nc, "setup") as ph:
        loaded, zeroed, built = ph.sem("loaded"), ph.sem("zeroed"), ph.sem("built")
        with nc.Block() as block:
            @block.sync
            def _(sp):
                sp.dma_start(X[:, :, :], x.rearrange("b (n p) d -> p (b n) d", p=P)).then_inc(loaded, 16)
                sp.wait_ge(loaded, 16)

            @block.gpsimd
            def _(pool):
                for t in (ident, ident_bf, mask_qk, mask_kq):
                    pool.memset(t[:, :], 0.0).then_inc(zeroed, 1)
                pool.wait_ge(zeroed, 4)
                for t in (ident, ident_bf):
                    pool.affine_select(out=t[:, :], in_=t[:, :], compare_op=ALU.not_equal, fill=1.0, base=0,
                                       pattern=[[-1, P]], channel_multiplier=1).then_inc(built, 1)
                pool.affine_select(out=mask_qk[:, :], in_=mask_qk[:, :], compare_op=ALU.is_ge, fill=NEG, base=0,
                                   pattern=[[-1, P]], channel_multiplier=1).then_inc(built, 1)
                pool.affine_select(out=mask_kq[:, :], in_=mask_kq[:, :], compare_op=ALU.is_ge, fill=NEG, base=0,
                                   pattern=[[1, P]], channel_multiplier=-1).then_inc(built, 1)


def normed(nc, name, X, ident, xn, second_eps=None, gain=None, shift=None):
    xhi, xlo = xn
    with Phase(nc, name) as ph:
        stats = ph.sb("stats", [P, NT, 6])
        mv = ph.sb("mv", [P, NT, 2])
        var_eps = ph.sb("var_eps", [P, NT])
        root = ph.sb("root", [P, NT])
        rstd = ph.sb("rstd", [P, NT])
        rstd2 = ph.sb("rstd2", [P, NT])
        xt = ph.sb("xt", [P, 2, TPC, D])
        cols = ph.sb("cols", [P, 2, KT])
        full = ph.sb("full", [P, 2, KT, CH])
        turned = [ph.psum(f"turned{u}", [P, KT, CH]) for u in range(2)]
        loaded, step, rooted = ph.sem("loaded"), ph.sem("step"), ph.sem("rooted")
        scaled, turn, hi_out, lo_out, fulls = (ph.sem(n) for n in ("scaled", "turn", "hi_out", "lo_out", "fulls"))
        affine = gain is not None
        with nc.Block() as block:
            @block.sync
            def _(sp):
                if affine:
                    for n, v in enumerate((gain, shift)):
                        sp.dma_start(cols[:, n, :], v).then_inc(loaded, 16)
                    sp.wait_ge(loaded, 32)

            @block.vector
            def _(dve):
                for t in range(NT):
                    dve.bn_stats(stats[:, t, :], X[:, t, :]).then_inc(step, 1)
                dve.wait_ge(step, NT)
                for t in range(NT):
                    dve.bn_aggr(mv[:, t, :], stats[:, t, :]).then_inc(step, 1)
                n = 2 * NT
                dve.wait_ge(step, n)
                dve.tensor_scalar(var_eps[:, :], mv[:, :, 1], LN_EPS, None, ALU.add).then_inc(step, 1)
                dve.wait_ge(rooted, 1)
                dve.reciprocal(rstd[:, :], root[:, :]).then_inc(step, 1)
                dve.wait_ge(step, n + 2)
                if second_eps is not None:
                    dve.tensor_tensor(rstd2[:, :], rstd[:, :], rstd[:, :], ALU.mult).then_inc(step, 1)
                    dve.wait_ge(step, n + 3)
                    dve.tensor_tensor(rstd2[:, :], rstd2[:, :], mv[:, :, 1], ALU.mult).then_inc(step, 1)
                    dve.wait_ge(step, n + 4)
                    dve.tensor_scalar(var_eps[:, :], rstd2[:, :], second_eps, None, ALU.add).then_inc(step, 1)
                    dve.wait_ge(rooted, 2)
                    dve.reciprocal(rstd2[:, :], root[:, :]).then_inc(step, 1)
                    dve.wait_ge(step, n + 6)
                    dve.tensor_tensor(rstd[:, :], rstd[:, :], rstd2[:, :], ALU.mult).then_inc(step, 1)
                    dve.wait_ge(step, n + 7)
                with dve.Fori(0, NCH // 2) as j:
                    for u in range(2):
                        dve.wait_ge(turn, two_back(2 * j + u))
                        for t in range(TPC):
                            tile = bass.ds(2 * TPC * j + (TPC * u + t), 1)
                            ins = dve.tensor_scalar(xt[:, u, t, :], X[:, tile, :], mv[:, tile, 0], rstd[:, tile],
                                                    ALU.subtract, ALU.mult)
                        ins.then_inc(scaled, 1)
                    for u in range(2):
                        dve.wait_ge(turn, cnth(2 * j + u))
                        if affine:
                            dve.wait_ge(fulls, nth(2 * j + u))
                            dve.tensor_copy(xhi[:, :, bass.ds(2 * CH * j + CH * u, CH)], full[:, u, :, :]).then_inc(hi_out, 1)
                        dve.wait_ge(hi_out, nth(2 * j + u))
                        src = full[:, u, :, :] if affine else turned[u][:, :, :]
                        at = bass.ds(2 * CH * j + CH * u, CH)
                        dve.tensor_tensor(xlo[:, :, at], src, f(xhi[:, :, at]), ALU.subtract).then_inc(lo_out, 1)

            @block.tensor
            def _(pe):
                pe.sem_inc(turn, 2)
                with pe.Fori(0, NCH // 2) as j:
                    for u in range(2):
                        pe.wait_ge(scaled, 2 * j + (u + 1))
                        pe.wait_ge(lo_out, two_back(2 * j + u))
                        for t in range(TPC):
                            for k in range(KT):
                                ins = pe.transpose(turned[u][:, k, t * P:(t + 1) * P],
                                                   xt[:, u, t, k * P:(k + 1) * P], ident[:, :])
                        ins.then_inc(turn, 1)

            @block.scalar
            def _(act):
                act.sem_inc(lo_out, 2)
                act.wait_ge(step, 2 * NT + 1)
                act.activation(root[:, :], var_eps[:, :], ACT.Sqrt).then_inc(rooted, 1)
                if second_eps is not None:
                    act.wait_ge(step, 2 * NT + 5)
                    act.activation(root[:, :], var_eps[:, :], ACT.Sqrt).then_inc(rooted, 1)
                if affine:
                    act.wait_ge(loaded, 32)
                with act.Fori(0, NCH // 2) as j:
                    for u in range(2):
                        act.wait_ge(turn, cnth(2 * j + u))
                        if affine:
                            act.wait_ge(lo_out, two_back(2 * j + u))
                            for k in range(KT):
                                ins = act.activation(full[:, u, k, :], turned[u][:, k, :], ACT.Identity,
                                                     bias=cols[:, 1, k:k + 1], scale=cols[:, 0, k:k + 1])
                            ins.then_inc(fulls, 1)
                        else:
                            act.activation(xhi[:, :, bass.ds(2 * CH * j + CH * u, CH)], turned[u][:, :, :],
                                           ACT.Copy).then_inc(hi_out, 1)


def qkv(nc, name, ident, xn, weights, dh, q_scr, k_scr, k_rows, V, v_cols,
        in_gain=None, q_bias=None, k_bias=None, v_bias=None, head_gain=None):
    xhi, xlo = xn
    width = max(b for _, b, _ in weights)
    nm = 4 if k_rows == P else 3
    quads = q_scr.shape[1] // B
    qg = P // (4 * dh)
    kh = k_scr.shape[2]
    with Phase(nc, name) as ph:
        stage = ph.sb("stage", [P, KT, width])
        whi, wlo = ph.sb("whi", [P, KT, width], F32R), ph.sb("wlo", [P, KT, width], F32R)
        gains = ph.sb("gains", [P, len(weights), KT])
        bias = ph.sb("bias", [P, nm])
        vb = ph.sb("vb", [P, v_cols])
        hg = ph.sb("hg", [P, 1])
        eps = ph.sb("eps", [P, 1])
        blocks = ph.sb("blocks", [P, P])
        qf = ph.sb("qf", [P, 2, CH])
        sq = ph.sb("sq", [P, 2, CH])
        qn = ph.sb("qn", [P, 2, CH])
        qhi, qlo = ph.sb("qhi", [P, 2, CH], F32R), ph.sb("qlo", [P, 2, CH], F32R)
        vx = ph.sb("vx", [P, 2, 2, KT, P], F32R)
        pq = ph.psum("pq", [P, 2, CH])
        pr = ph.psum("pr", [P, 2, CH])
        pv = ph.psum("pv", [P, 2, CH])
        loaded, wgain, whi_ok, wlo_ok = (ph.sem(n) for n in ("loaded", "wgain", "whi_ok", "wlo_ok"))
        projected, biased, squared, summed, logged, inverted, headed, cut_hi, cut_lo = (
            ph.sem(n) for n in ("projected", "biased", "squared", "summed", "logged", "inverted", "headed",
                                "cut_hi", "cut_lo"))
        stored = [ph.sem(f"stored{h}") for h in range(2)]
        blocked, vcopy, vmul, vout = (ph.sem(n) for n in ("blocked", "vcopy", "vmul", "vout"))
        steps = nm * NCH
        rms = head_gain is not None
        loads = []
        for a, b, w in weights:
            loads.append((stage[:, :, a:b], w.rearrange("(k p) n -> p k n", p=P)))
        if in_gain is not None:
            for n, g in enumerate(in_gain):
                loads.append((gains[:, n, :], g))
        if q_bias is not None:
            loads.append((bias[:, 0:KT], q_bias))
            loads.append((bias[:, KT:2 * KT], k_bias[:, 0:KT]))
            loads.append((vb[:, :], v_bias.partition_broadcast(P)))
        if rms:
            for h in range(P // dh):
                loads.append((hg[h * dh:(h + 1) * dh, :], head_gain.rearrange("(p o) -> p o", o=1)))
        everything = 16 * len(loads)
        with nc.Block() as block:
            @block.sync
            def _(sp):
                for dst, src in loads:
                    sp.dma_start(dst, src).then_inc(loaded, 16)
                for h in range(2):
                    sp.sem_inc(stored[h], 32)
                with sp.Fori(0, B) as b:
                    for u in range(2):
                        for m in range(nm):
                            n = u * nm + m
                            sp.wait_ge(cut_lo, cnth(2 * nm * b + n))
                            for part, t in enumerate((qhi, qlo)):
                                cs = slice(u * CH, (u + 1) * CH)
                                if m < 2:
                                    dst = q_scr[part, bass.ds(quads * b + qg * m, qg), :, :, cs]
                                elif k_rows == P:
                                    dst = k_scr[part, bass.ds(quads * b + qg * (m - 2), qg), :, :, cs]
                                else:
                                    dst = k_scr[part, bass.ds(quads * b, quads), :, :, cs]
                                rows = P if m < 2 else k_rows
                                sp.dma_start(dst.rearrange("g h p n -> (g h p) n"),
                                             f(t[0:rows, n % 2, :])).then_inc(stored[n % 2], 16)
                for h in range(2):
                    sp.wait_ge(stored[h], 32 + 32 * steps // 2)

            @block.gpsimd
            def _(pool):
                if rms:
                    pool.memset(eps[:, :], RMS_EPS).then_inc(blocked, 1)
                    pool.memset(blocks[:, :], 1.0).then_inc(blocked, 1)
                    view = blocks[:, :].rearrange("p (h e) -> p h e", e=dh)
                    pool.wait_ge(blocked, 2)
                    pool.affine_select(out=view, in_=view, compare_op=ALU.is_ge, fill=0.0, base=0,
                                       pattern=[[-dh, P // dh], [0, dh]], channel_multiplier=1).then_inc(blocked, 1)
                    pool.wait_ge(blocked, 3)
                    pool.affine_select(out=view, in_=view, compare_op=ALU.is_ge, fill=0.0, base=dh - 1,
                                       pattern=[[dh, P // dh], [0, dh]], channel_multiplier=-1).then_inc(blocked, 1)
                for b in range(B):
                    with pool.Fori(0, ST // 2) as j:
                        for u in range(2):
                            pool.wait_ge(vmul, two_back(2 * j + (b * ST + u)))
                            at = bass.ds(2 * P * j + (b * S + u * P), P)
                            pool.tensor_copy(vx[:, u, 0, :, :], f(xhi[:, :, at]))
                            pool.tensor_copy(vx[:, u, 1, :, :], f(xlo[:, :, at])).then_inc(vcopy, 1)

            @block.tensor
            def _(pe):
                pe.sem_inc(vmul, CREDIT)
                pe.wait_ge(wlo_ok, len(weights))
                with pe.Fori(0, B) as b:
                    for u in range(2):
                        at = bass.ds(2 * CH * b + u * CH, CH)
                        for m in range(nm):
                            n = u * nm + m
                            pe.wait_ge(biased, two_back(2 * nm * b + n))
                            cs = slice(m * P, (m + 1) * P)
                            three_terms(pe, pq[:, n % 2, :],
                                        [((whi[:, k, cs], wlo[:, k, cs]), (xhi[:, k, at], xlo[:, k, at]))
                                         for k in range(KT)]).then_inc(projected, 1)
                            if rms:
                                if n == 0:
                                    pe.wait_ge(blocked, 4)
                                pe.wait_ge(squared, nth(2 * nm * b + n))
                                pe.matmul(pr[:, n % 2, :], blocks[:, :], sq[:, n % 2, :],
                                          start=True, stop=True).then_inc(summed, 1)
                for b in range(B):
                    with pe.Fori(0, ST // 2) as j:
                        for u in range(2):
                            n = 2 * j + (b * ST + u)
                            pe.wait_ge(vcopy, nth(n))
                            pe.wait_ge(vout, two_back(n))
                            three_terms(pe, pv[:, u, 0:D],
                                        [((vx[:, u, 0, k, :], vx[:, u, 1, k, :]),
                                          (whi[:, k, width - D:width], wlo[:, k, width - D:width]))
                                         for k in range(KT)]).then_inc(vmul, 1)

            @block.scalar
            def _(act):
                act.sem_inc(biased, CREDIT)
                for n, (a, b, _) in enumerate(weights):
                    if in_gain is None:
                        act.wait_ge(loaded, everything)
                    else:
                        act.wait_ge(wgain, n + 1)
                    act.activation(whi[:, :, a:b], stage[:, :, a:b], ACT.Copy).then_inc(whi_ok, 1)
                with act.Fori(0, B) as b:
                    for u in range(2):
                        for m in range(nm):
                            n = u * nm + m
                            h, step = n % 2, 2 * nm * b + n
                            act.wait_ge(projected, nth(step))
                            act.wait_ge(cut_lo, two_back(step))
                            if q_bias is not None:
                                act.activation(qf[:, h, :], pq[:, h, :], ACT.Identity,
                                               bias=bias[:, m:m + 1]).then_inc(biased, 1)
                            else:
                                act.activation(qf[:, h, :], pq[:, h, :], ACT.Copy).then_inc(biased, 1)
                            if rms:
                                act.wait_ge(biased, cnth(step))
                                act.activation(sq[:, h, :], qf[:, h, :], ACT.Square).then_inc(squared, 1)
                                if n == 0:
                                    act.wait_ge(blocked, 4)
                                act.wait_ge(summed, nth(step))
                                act.activation(sq[:, h, :], pr[:, h, :], ACT.Ln, bias=eps[:, :],
                                               scale=1.0 / dh).then_inc(logged, 1)
                                act.wait_ge(logged, nth(step))
                                act.activation(qn[:, h, :], sq[:, h, :], ACT.Exp, scale=-0.5).then_inc(inverted, 1)

            @block.vector
            def _(dve):
                dve.sem_inc(cut_lo, CREDIT)
                dve.sem_inc(vout, CREDIT)
                dve.wait_ge(loaded, everything)
                for n, (a, b, _) in enumerate(weights):
                    if in_gain is not None:
                        for k in range(KT):
                            ins = dve.tensor_scalar(stage[:, k, a:b], stage[:, k, a:b], gains[:, n, k:k + 1],
                                                    None, ALU.mult)
                        ins.then_inc(wgain, 1)
                    dve.wait_ge(whi_ok, n + 1)
                    if in_gain is not None:
                        dve.wait_ge(wgain, n + 1)
                    dve.tensor_tensor(wlo[:, :, a:b], stage[:, :, a:b], f(whi[:, :, a:b]),
                                      ALU.subtract).then_inc(wlo_ok, 1)
                with dve.Fori(0, B) as b:
                    for u in range(2):
                        for m in range(nm):
                            n = u * nm + m
                            h, step = n % 2, 2 * nm * b + n
                            dve.wait_ge(stored[h], 32 * nm * b + 32 * (n // 2 + 1))
                            if rms:
                                dve.wait_ge(inverted, nth(step))
                                dve.scalar_tensor_tensor(out=qf[:, h, :], in0=qf[:, h, :], scalar=hg[:, :],
                                                         in1=qn[:, h, :], op0=ALU.mult,
                                                         op1=ALU.mult).then_inc(headed, 1)
                                dve.wait_ge(headed, nth(step))
                            else:
                                dve.wait_ge(biased, cnth(step))
                            dve.tensor_copy(qhi[:, h, :], qf[:, h, :]).then_inc(cut_hi, 1)
                            dve.wait_ge(cut_hi, nth(step))
                            dve.tensor_tensor(qlo[:, h, :], qf[:, h, :], f(qhi[:, h, :]),
                                              ALU.subtract).then_inc(cut_lo, 1)
                for b in range(B):
                    with dve.Fori(0, ST // 2) as j:
                        for u in range(2):
                            dve.wait_ge(vmul, cnth(2 * j + (b * ST + u)))
                            dst = V[:, b * quads:(b + 1) * quads, bass.ds(2 * j + u, 1), :]
                            dst = dst.rearrange("p g o c -> p g (o c)")
                            src = pv[:, u, D - v_cols:D].rearrange("p (g c) -> p g c", g=quads)
                            if v_bias is not None:
                                dve.tensor_tensor(dst, src, vb[:, :].rearrange("p (g c) -> p g c", g=quads),
                                                  ALU.add).then_inc(vout, 1)
                            else:
                                dve.tensor_copy(dst, src).then_inc(vout, 1)


def attention(nc, name, q_scr, k_scr, V, O, ident, ident_bf, mask_qk, mask_kq, dh, scale, causal):
    NQ = q_scr.shape[1]
    kh = k_scr.shape[2]
    units = [(c, kt) for c in range(2) for kt in range(TPC * (c + 1) if causal else ST)]
    chunks = [(h, qt, kc) for h in range(4) for qt in range(ST) for kc in range(2)
              if not causal or kc * CH < (qt + 1) * P]
    nu, n1 = len(units), len(chunks) + 1
    FIRST, LAST = 2, nu - 2
    mrow = 3 * dh

    def span(c, kt):
        q0 = P * (kt - TPC * c) if causal and kt >= TPC * c else 0
        return q0, min(q0, CH - 2 * P)

    with Phase(nc, name) as ph:
        Q = [ph.sb(f"Q{u}", [P, 4, S], F32R) for u in range(2)]
        K = [ph.sb(f"K{u}", [P, kh, S], F32R) for u in range(2)]
        VS = [ph.sb(f"VS{u}", [P, ST, kh, 32]) for u in range(2)]
        PR = ph.sb("PR", [P, 4, 4, CH])
        mxp = ph.sb("mxp", [P, 4, ST, 2])
        nmax = ph.sb("nmax", [P, 4 * ST])
        mhi = ph.sb("mhi", [4 * ST, 2, P], F32R)
        mlo = ph.sb("mlo", [4 * ST, 2, P], F32R)
        OT = ph.sb("OT", [P, 2, CH])
        rec = ph.sb("rec", [P, 2, TPC, 4])
        s1 = ph.psum("s1", [P, 2, CH])
        s2 = ph.psum("s2", [P, 4, CH])
        o = ph.psum("o", [P, 2, CH])
        cleared, qk_in, m_in, vs_in = (ph.sem(n) for n in ("cleared", "qk_in", "m_in", "vs_in"))
        mxp_set = ph.sem("mxp_set")
        s1_full, s1_free, m_red, mhi_ok = (ph.sem(n) for n in ("s1_full", "s1_free", "m_red", "mhi_ok"))
        s2_full, p_ready, pv_done = (ph.sem(n) for n in ("s2_full", "p_ready", "pv_done"))
        ot_ready, ox_full, recd, o_free = (ph.sem(n) for n in ("ot_ready", "ox_full", "recd", "o_free"))
        loads_per_quad = 16 * 7

        def over_quads(eng, quad):
            with eng.Fori(0, NQ // 2 - 1) as j:
                quad(2 * j, 0, False)
                quad(2 * j + 1, 1, False)
            quad(NQ - 2, 0, False)
            quad(NQ - 1, 1, True)

        with nc.Block() as block:
            @block.sync
            def _(sp):
                def load(i, u):
                    for part, row in ((0, 0), (1, dh), (0, 2 * dh)):
                        sp.dma_start(f(Q[u][row:row + dh, :, :]),
                                     q_scr[part, bass.ds(i, 1)].rearrange("o h p n -> p (o h) n")).then_inc(qk_in, 16)
                    sp.dma_start(f(Q[u][mrow:mrow + 2, :, :]), f(Q[u][ROWS - 2:ROWS, :, :])).then_inc(qk_in, 16)
                    for part, row in ((0, 0), (0, dh), (1, 2 * dh)):
                        sp.dma_start(f(K[u][row:row + dh, :, :]),
                                     k_scr[part, bass.ds(i, 1)].rearrange("o h p n -> p (o h) n")).then_inc(qk_in, 16)

                def maxima(i, u):
                    sp.wait_ge(s1_free, n1 * (i + 1))
                    sp.dma_start(f(Q[u][mrow:mrow + 1, :, :]), f(mhi[:, u, :])).then_inc(m_in, 16)
                    sp.dma_start(f(Q[u][mrow + 1:mrow + 2, :, :]), f(mlo[:, u, :])).then_inc(m_in, 16)

                def quad(i, u, last):
                    if not last:
                        maxima(i + 1, 1 - u)
                        if not (isinstance(i, int) and i == NQ - 2):
                            sp.wait_ge(s2_full, 2 * nu * (i + 1))
                            load(i + 2, u)

                sp.wait_ge(cleared, 6)
                load(0, 0)
                load(1, 1)
                maxima(0, 0)
                over_quads(sp, quad)

            @block.gpsimd
            def _(pool):
                for u in range(2):
                    pool.memset(Q[u][:, :, :].bitcast(F32), 0.0).then_inc(cleared, 1)
                    pool.memset(K[u][:, :, :].bitcast(F32), 1.0).then_inc(cleared, 1)
                for u in range(2):
                    pool.memset(VS[u][:, :, :, :], 0.0).then_inc(cleared, 1)
                pool.wait_ge(cleared, 6)
                for u in range(2):
                    pool.memset(VS[u][:, :, :, dh:dh + 1], 1.0).then_inc(cleared, 1)
                pool.wait_ge(cleared, 8)

                def values(i, u):
                    src = V[:, bass.ds(i, 1), :, :].rearrange("p o k (h c) -> p (o k) h c", h=kh)
                    pool.tensor_copy(VS[u][:, :, :, 0:dh], src).then_inc(vs_in, 1)

                values(0, 0)
                values(1, 1)
                with pool.Fori(0, NQ // 2 - 1) as j:
                    for u in range(2):
                        pool.wait_ge(pv_done, 4 + nu * (2 * j + (u + 1)))
                        values(2 * j + (u + 2), u)

            @block.tensor
            def _(pe):
                def scores1(i, u, n):
                    h, qt, kc = chunks[n]
                    if not (isinstance(i, int) and i == 0 and n < 2):
                        pe.wait_ge(s1_free, n1 * i + (n - 1))
                    slot = (u * n1 + n) % 2
                    cols = min(CH, (qt + 1) * P - kc * CH) if causal else CH
                    wide = max(cols, 2 * P)
                    diagonal = causal and (qt + 1) * P <= (kc + 1) * CH
                    ins = pe.matmul(s1[:, slot, 0:wide], Q[u][0:ROWS, h, qt * P:(qt + 1) * P],
                                    K[u][0:ROWS, h % kh, kc * CH:kc * CH + wide], start=True, stop=not diagonal)
                    if diagonal:
                        ins = pe.matmul(s1[:, slot, cols - P:cols], ident_bf[:, :], mask_qk[:, :],
                                        start=False, stop=True)
                    ins.then_inc(s1_full, 1)

                def turn_maxima(i, u):
                    pe.wait_ge(m_red, nth(i))
                    pe.wait_ge(s1_free, n1 * i + (n1 - 2))
                    slot = (u * n1 + n1 - 1) % 2
                    pe.transpose(s1[0:4 * ST, slot, 0:P], nmax[:, :], ident[:, :]).then_inc(s1_full, 1)

                def scores2(i, u, n):
                    c, kt = units[n]
                    q0, first = span(c, kt)
                    diagonal = causal and kt >= TPC * c
                    for half in range(2):
                        pe.wait_ge(p_ready, two_back(2 * nu * i + (2 * n + half)))
                        for h in (2 * half, 2 * half + 1):
                            ins = pe.matmul(s2[:, h, first:CH], K[u][0:ROWS, h % kh, kt * P:(kt + 1) * P],
                                            Q[u][0:ROWS, h, c * CH + first:(c + 1) * CH],
                                            start=True, stop=not diagonal)
                            if diagonal:
                                ins = pe.matmul(s2[:, h, q0:q0 + P], ident_bf[:, :], mask_kq[:, :],
                                                start=False, stop=True)
                        ins.then_inc(s2_full, 1)

                def product(i, u, n):
                    c, kt = units[n]
                    q0, _ = span(c, kt)
                    lastkt = n == nu - 1 or units[n + 1][0] != c
                    pe.wait_ge(p_ready, cnth(2 * nu * i + (2 * n + 1)))
                    if kt == 0:
                        pe.wait_ge(o_free, two_back(2 * i + c))
                    for h in range(4):
                        ins = pe.matmul(o[32 * h:32 * h + 32, c, q0:CH], VS[u][:, kt, h % kh, :],
                                        PR[:, n % 4, h, q0:CH], start=kt == 0, stop=lastkt)
                    ins.then_inc(pv_done, 1)

                def turn_outputs(i, c):
                    pe.wait_ge(ot_ready, nth(2 * i + c))
                    for t in range(TPC):
                        ins = pe.transpose(o[:, c, t * P:(t + 1) * P], OT[:, c, t * P:(t + 1) * P], ident[:, :])
                    ins.then_inc(ox_full, 1)

                def quad(i, u, last):
                    pe.wait_ge(vs_in, nth(i))
                    pe.wait_ge(m_in, 32 * (i + 1))
                    nxt = 0
                    for n in range(nu):
                        scores2(i, u, n)
                        if not last and n >= FIRST:
                            if n == FIRST:
                                pe.wait_ge(qk_in, loads_per_quad * (i + 2))
                            upto = min(len(chunks), -(-len(chunks) * (n - FIRST + 1) // (LAST - FIRST)))
                            for m in range(nxt, upto):
                                scores1(i + 1, 1 - u, m)
                            nxt = upto
                        if n == LAST and not last:
                            turn_maxima(i + 1, 1 - u)
                        if n >= 1:
                            product(i, u, n - 1)
                        if n >= 2 and units[n - 2][0] == 0 and units[n - 1][0] == 1:
                            turn_outputs(i, 0)
                    product(i, u, nu - 1)
                    turn_outputs(i, 1)

                pe.sem_inc(pv_done, 4)
                pe.wait_ge(cleared, 8)
                pe.wait_ge(qk_in, 2 * loads_per_quad)
                for n in range(len(chunks)):
                    scores1(0, 0, n)
                turn_maxima(0, 0)
                over_quads(pe, quad)

            @block.scalar
            def _(act):
                act.sem_inc(p_ready, CREDIT)

                def quad(i, u, last):
                    for n, (c, kt) in enumerate(units):
                        q0, _ = span(c, kt)
                        act.wait_ge(pv_done, nu * i + (n + 1))
                        for half in range(2):
                            act.wait_ge(s2_full, 2 * nu * i + (2 * n + half + 1))
                            hs = slice(2 * half, 2 * half + 2)
                            act.activation(PR[:, n % 4, hs, q0:CH], s2[:, hs, q0:CH], ACT.Exp,
                                           scale=scale).then_inc(p_ready, 1)

                over_quads(act, quad)

            @block.vector
            def _(dve):
                def maximum(i, u, n):
                    h, qt, kc = chunks[n]
                    slot = (u * n1 + n) % 2
                    cols = min(CH, (qt + 1) * P - kc * CH) if causal else CH
                    dve.wait_ge(s1_full, n1 * i + (n + 1))
                    dve.tensor_reduce(mxp[:, h, qt, kc:kc + 1], s1[:, slot, 0:cols], AX.X, ALU.max).then_inc(s1_free, 1)

                def maxima(i, u):
                    dve.wait_ge(s1_free, n1 * i + (n1 - 1))
                    dve.tensor_reduce(nmax[:, :], mxp[:, :, :, :].rearrange("p h q k -> p (h q) k"), AX.X, ALU.max,
                                      negate=True).then_inc(m_red, 1)
                    slot = (u * n1 + n1 - 1) % 2
                    dve.wait_ge(s1_full, n1 * (i + 1))
                    if not (isinstance(i, int) and i < 2):
                        dve.wait_ge(m_in, 32 * i)
                    dve.tensor_copy(mhi[:, u, :], s1[0:4 * ST, slot, 0:P]).then_inc(mhi_ok, 1)
                    dve.wait_ge(mhi_ok, nth(i))
                    dve.tensor_tensor(mlo[:, u, :], s1[0:4 * ST, slot, 0:P], f(mhi[:, u, :]),
                                      ALU.subtract).then_inc(s1_free, 1)

                def outputs(i, c):
                    dve.wait_ge(pv_done, 4 + nu * i + (sum(a <= c for a, _ in units)))
                    dve.tensor_copy(OT[:, c, :], o[:, c, :]).then_inc(ot_ready, 1)

                def normalised(i, c):
                    dve.wait_ge(ox_full, nth(2 * i + c))
                    turned = o[:, c, :].rearrange("p (t h e) -> p t h e", t=TPC, h=4)
                    dve.reciprocal(rec[:, c, :, :], turned[:, :, :, dh]).then_inc(recd, 1)
                    dve.wait_ge(recd, nth(2 * i + c))
                    for t in range(TPC):
                        dst = O[:, c * TPC + t, bass.ds(i, 1), :].rearrange("p o (h e) -> p (o h) e", h=4)
                        ins = dve.tensor_tensor(dst, turned[:, t, :, 0:dh],
                                                rec[:, c, t, :].unsqueeze(2).broadcast_to([P, 4, dh]), ALU.mult)
                    ins.then_inc(o_free, 1)

                def quad(i, u, last):
                    nxt = 0
                    for n in range(nu):
                        if not last and n >= FIRST:
                            upto = min(len(chunks), -(-len(chunks) * (n - FIRST + 1) // (LAST - FIRST)))
                            for m in range(nxt, upto):
                                maximum(i + 1, 1 - u, m)
                            nxt = upto
                        if n == LAST and not last:
                            maxima(i + 1, 1 - u)
                        if n >= 2 and units[n - 2][0] == 0 and units[n - 1][0] == 1:
                            normalised(i, 0)
                        if n >= 1 and units[n - 1][0] == 0 and units[n][0] == 1:
                            outputs(i, 0)
                    outputs(i, 1)
                    normalised(i, 1)

                dve.sem_inc(o_free, CREDIT)
                dve.memset(mxp[:, :, :, :], NEG).then_inc(mxp_set, 1)
                dve.wait_ge(mxp_set, 1)
                for n in range(len(chunks)):
                    maximum(0, 0, n)
                maxima(0, 0)
                over_quads(dve, quad)


def out_projection(nc, name, X, O, ident, w, bias=None):
    quads = O.shape[2] // B
    with Phase(nc, name) as ph:
        stage = ph.sb("stage", [P, KT, D])
        whi, wlo = ph.sb("whi", [P, KT, D], F32R), ph.sb("wlo", [P, KT, D], F32R)
        bb = ph.sb("bb", [P, D])
        ohi, olo = ph.sb("ohi", [P, 2, KT, P], F32R), ph.sb("olo", [P, 2, KT, P], F32R)
        turned = ph.psum("turned", [P, 2, CH])
        py = ph.psum("py", [P, 2, CH])
        loaded, whi_ok, wlo_ok, added = (ph.sem(n) for n in ("loaded", "whi_ok", "wlo_ok", "added"))
        turn, hi_ok, lo_ok, mul, out = (ph.sem(n) for n in ("turn", "hi_ok", "lo_ok", "mul", "out"))
        with nc.Block() as block:
            @block.sync
            def _(sp):
                sp.dma_start(stage[:, :, :], w.rearrange("(k p) n -> p k n", p=P)).then_inc(loaded, 16)
                if bias is not None:
                    sp.dma_start(bb[:, :], bias.partition_broadcast(P)).then_inc(loaded, 16)

            @block.tensor
            def _(pe):
                def turned_tile(n):
                    b, t = n // ST, n % ST
                    if n >= 2:
                        pe.wait_ge(lo_ok, n - 1)
                    for k in range(KT):
                        src = O[:, t, b * quads + k * quads // KT:b * quads + (k + 1) * quads // KT, :]
                        ins = pe.transpose(turned[:, n % 2, k * P:(k + 1) * P], src.rearrange("p g c -> p (g c)"), ident[:, :])
                    ins.then_inc(turn, 1)

                turned_tile(0)
                for n in range(NT):
                    if n + 1 < NT:
                        turned_tile(n + 1)
                    if n == 0:
                        pe.wait_ge(wlo_ok, 1)
                    pe.wait_ge(lo_ok, n + 1)
                    if n >= 2:
                        pe.wait_ge(out, n - 1)
                    three_terms(pe, py[:, n % 2, 0:D],
                                [((ohi[:, n % 2, k, :], olo[:, n % 2, k, :]), (whi[:, k, :], wlo[:, k, :]))
                                 for k in range(KT)]).then_inc(mul, 1)

            @block.scalar
            def _(act):
                act.wait_ge(loaded, 32 if bias is not None else 16)
                act.activation(whi[:, :, :], stage[:, :, :], ACT.Copy).then_inc(whi_ok, 1)
                for n in range(NT):
                    act.wait_ge(turn, n + 1)
                    if n >= 2:
                        act.wait_ge(mul, n - 1)
                    act.activation(ohi[:, n % 2, :, :].rearrange("p k n -> p (k n)"), turned[:, n % 2, 0:D],
                                   ACT.Copy).then_inc(hi_ok, 1)

            @block.vector
            def _(dve):
                dve.wait_ge(whi_ok, 1)
                dve.tensor_tensor(wlo[:, :, :], stage[:, :, :], f(whi[:, :, :]), ALU.subtract).then_inc(wlo_ok, 1)
                if bias is not None:
                    for t in range(NT):
                        ins = dve.tensor_tensor(X[:, t, :], X[:, t, :], bb[:, :], ALU.add)
                    ins.then_inc(added, 1)
                    dve.wait_ge(added, 1)

                def summed(n):
                    dve.wait_ge(mul, n + 1)
                    dve.tensor_tensor(X[:, n, :], py[:, n % 2, 0:D], X[:, n, :], ALU.add).then_inc(out, 1)

                for n in range(NT):
                    dve.wait_ge(hi_ok, n + 1)
                    dve.tensor_tensor(olo[:, n % 2, :, :].rearrange("p k n -> p (k n)"), turned[:, n % 2, 0:D],
                                      f(ohi[:, n % 2, :, :]).rearrange("p k n -> p (k n)"),
                                      ALU.subtract).then_inc(lo_ok, 1)
                    if n >= 1:
                        summed(n - 1)
                summed(NT - 1)


def gated_ffn(nc, name, X, xn, ident, w1, w2, rest, gate_w=None):
    xhi, xlo = xn
    E = w1.shape[0]
    W1 = w1.shape[2]
    K2 = 2 if rest else 1
    tiles = 3 if rest else 2
    UO = 64
    EX = E - 1
    with Phase(nc, name) as ph:
        w1hi, w1lo = ph.sb("w1hi", [P, E, KT, W1], F32R), ph.sb("w1lo", [P, E, KT, W1], F32R)
        w2hi, w2lo = ph.sb("w2hi", [P, E, K2, D], F32R), ph.sb("w2lo", [P, E, K2, D], F32R)
        st1 = ph.sb("st1", [P, 2, KT, W1])
        st2 = ph.sb("st2", [P, 2, K2, D])
        sg = ph.sb("sg", [P, 2, 2, CH])
        hf = ph.sb("hf", [P, 2, K2, CH])
        hhi, hlo = ph.sb("hhi", [P, 2, K2, CH], F32R), ph.sb("hlo", [P, 2, K2, CH], F32R)
        pg = [ph.psum(f"pg{u}", [P, 3, CH]) for u in range(2)]
        py = ph.psum("py", [P, TPC, D])
        loaded = [ph.sem(f"loaded{u}") for u in range(2)]
        whi_ok, wlo_ok, zeroed = (ph.sem(n) for n in ("whi_ok", "wlo_ok", "zeroed"))
        g_full, sg_ok, h_ok, hi_ok, lo_ok, y_full, y_out = (
            ph.sem(n) for n in ("g_full", "sg_ok", "h_ok", "hi_ok", "lo_ok", "y_full", "y_out"))
        if gate_w is not None:
            gst = ph.sb("gst", [P, KT, EX])
            ghi, glo = ph.sb("ghi", [P, KT, P], F32R), ph.sb("glo", [P, KT, P], F32R)
            lt = ph.sb("lt", [EX, NCH, CH])
            lg = ph.sb("lg", [P, NT, EX])
            small = ph.sb("small", [P, 2, NT])
            top = ph.sb("top", [P, NT, 8])
            topi = ph.sb("topi", [P, NT, 8], mybir.dt.uint32)
            topf = ph.sb("topf", [P, NT, 2])
            number = ph.sb("number", [P, NT, EX])
            chosen = ph.sb("chosen", [P, 2, NT, EX])
            cw = ph.sb("cw", [P, NT, E])
            gated, gcut, gmul, glt, gturn, gs, gexp = (
                ph.sem(n) for n in ("gated", "gcut", "gmul", "glt", "gturn", "gs", "gexp"))
        with nc.Block() as block:
            @block.sync
            def _(sp):
                if gate_w is not None:
                    sp.dma_start(gst[:, :, :], gate_w.rearrange("(k p) e -> p k e", p=P)).then_inc(gated, 16)
                for e in range(E):
                    if e >= 2:
                        sp.wait_ge(wlo_ok, e - 1)
                    sp.dma_start(st1[:, e % 2, :, :], w1[e].rearrange("(k p) n -> p k n", p=P)).then_inc(loaded[e % 2], 16)
                    sp.dma_start(st2[:, e % 2, :, :], w2[e].rearrange("k p n -> p k n")).then_inc(loaded[e % 2], 16)

            @block.gpsimd
            def _(pool):
                if rest:
                    pool.memset(hhi[:, :, 1, :].bitcast(F32), 0.0).then_inc(zeroed, 1)
                    pool.memset(hlo[:, :, 1, :].bitcast(F32), 0.0).then_inc(zeroed, 1)
                if gate_w is not None:
                    pool.memset(ghi[:, :, :].bitcast(F32), 0.0).then_inc(zeroed, 1)
                    pool.memset(glo[:, :, :].bitcast(F32), 0.0).then_inc(zeroed, 1)
                    pool.memset(cw[:, :, :], 1.0).then_inc(zeroed, 1)

            @block.tensor
            def _(pe):
                if gate_w is not None:
                    pe.wait_ge(gcut, 2)
                    for c in range(NCH):
                        at = slice(c * CH, (c + 1) * CH)
                        three_terms(pe, pg[c % 2][:, c // 2, :],
                                    [((ghi[:, k, :], glo[:, k, :]), (xhi[:, k, at], xlo[:, k, at]))
                                     for k in range(KT)]).then_inc(gmul, 1)
                    pe.wait_ge(glt, NCH)
                    for t in range(NT):
                        ins = pe.transpose(pg[0][:, 2, t * EX:(t + 1) * EX], lt[:, t // TPC, (t % TPC) * P:(t % TPC + 1) * P],
                                           ident[0:EX, 0:EX])
                    ins.then_inc(gturn, 1)
                    pe.wait_ge(gs, 1)

                def hidden(j, k):
                    n, e = 2 * E * j + k, k % E
                    at = bass.ds(2 * CH * j + CH * (k // E), CH)
                    if k < E:
                        pe.wait_ge(wlo_ok, e + 1)
                    pe.wait_ge(h_ok, two_back(n))
                    for m in range(tiles):
                        cs = slice(m * P, (m + 1) * P) if m < 2 else slice(2 * P, W1)
                        ins = three_terms(pe, pg[k % 2][0:cs.stop - cs.start, m, :],
                                          [((w1hi[:, e, q, cs], w1lo[:, e, q, cs]), (xhi[:, q, at], xlo[:, q, at]))
                                           for q in range(KT)])
                    ins.then_inc(g_full, 1)

                def down(j, k):
                    n, e = 2 * E * j + k, k % E
                    pe.wait_ge(lo_ok, nth(n))
                    pe.wait_ge(y_out, nth(n))
                    if rest:
                        pe.wait_ge(zeroed, 2)
                    for t in range(TPC):
                        ts = slice(t * P, (t + 1) * P)
                        ins = three_terms(pe, py[:, t, :],
                                          [((hhi[0:(P, ROWS)[q], k % 2, q, ts], hlo[0:(P, ROWS)[q], k % 2, q, ts]),
                                            (w2hi[0:(P, ROWS)[q], e, q, :], w2lo[0:(P, ROWS)[q], e, q, :]))
                                           for q in range(K2)])
                    ins.then_inc(y_full, 1)

                pe.sem_inc(y_full, CREDIT)
                with pe.Fori(0, NCH // 2) as j:
                    for k in range(2 * E):
                        hidden(j, k)
                        if k >= 1:
                            down(j, k - 1)
                    down(j, 2 * E - 1)

            @block.scalar
            def _(act):
                if gate_w is not None:
                    act.wait_ge(gs, 2)
                    act.activation(lg[:, :, :], lg[:, :, :], ACT.Exp).then_inc(gexp, 1)
                for e in range(E):
                    act.wait_ge(loaded[e % 2], 32 * (e // 2 + 1))
                    act.activation(w1hi[:, e, :, :], st1[:, e % 2, :, :], ACT.Copy)
                    act.activation(w2hi[:, e, :, :], st2[:, e % 2, :, :], ACT.Copy).then_inc(whi_ok, 1)
                if rest:
                    act.wait_ge(zeroed, 2)
                with act.Fori(0, NCH // 2) as j:
                    for k in range(2 * E):
                        n, h = 2 * E * j + k, k % 2
                        act.wait_ge(g_full, nth(n))
                        act.wait_ge(h_ok, two_back(n))
                        ins = act.activation(sg[:, h, 0, :], pg[h][:, 0, :], ACT.Silu)
                        if rest:
                            ins = act.activation(sg[UO:UO + 48, h, 1, :], pg[h][0:48, 2, :], ACT.Silu)
                        ins.then_inc(sg_ok, 1)
                        act.wait_ge(h_ok, cnth(n))
                        act.wait_ge(y_full, two_back(n))
                        ins = act.activation(hhi[:, h, 0, :], hf[:, h, 0, :], ACT.Copy)
                        if rest:
                            ins = act.activation(hhi[0:48, h, 1, :], hf[0:48, h, 1, :], ACT.Copy)
                        ins.then_inc(hi_ok, 1)

            @block.vector
            def _(dve):
                if gate_w is not None:
                    dve.wait_ge(gated, 16)
                    dve.wait_ge(zeroed, 5 if rest else 3)
                    dve.tensor_copy(ghi[:, :, 0:EX], gst[:, :, :]).then_inc(gcut, 1)
                    dve.wait_ge(gcut, 1)
                    dve.tensor_tensor(glo[:, :, 0:EX], gst[:, :, :], f(ghi[:, :, 0:EX]), ALU.subtract).then_inc(gcut, 1)
                    for c in range(NCH):
                        dve.wait_ge(gmul, c + 1)
                        dve.tensor_copy(lt[:, c, :], pg[c % 2][0:EX, c // 2, :]).then_inc(glt, 1)
                    dve.wait_ge(gturn, 1)
                    dve.tensor_copy(lg[:, :, :], pg[0][:, 2, 0:NT * EX].rearrange("p (t e) -> p t e", e=EX)).then_inc(gs, 1)
                    dve.wait_ge(gs, 1)
                    dve.tensor_reduce(small[:, 0, :], lg[:, :, :], AX.X, ALU.max).then_inc(gcut, 1)
                    dve.wait_ge(gcut, 3)
                    wide = lambda v: v.unsqueeze(2).broadcast_to([P, NT, EX])
                    dve.tensor_tensor(lg[:, :, :], lg[:, :, :], wide(small[:, 0, :]), ALU.subtract).then_inc(gs, 1)
                    dve.wait_ge(gexp, 1)
                    dve.tensor_reduce(small[:, 0, :], lg[:, :, :], AX.X, ALU.add).then_inc(gcut, 1)
                    dve.wait_ge(gcut, 4)
                    dve.reciprocal(small[:, 1, :], small[:, 0, :]).then_inc(gcut, 1)
                    dve.wait_ge(gcut, 5)
                    dve.tensor_tensor(lg[:, :, :], lg[:, :, :], wide(small[:, 1, :]), ALU.mult).then_inc(gcut, 1)
                    dve.wait_ge(gcut, 6)
                    for t in range(NT):
                        ins = dve.max(top[:, t, :], lg[:, t, :])
                    ins.then_inc(gcut, 1)
                    dve.wait_ge(gcut, 7)
                    dve.tensor_tensor(small[:, 0, :], top[:, :, 0], top[:, :, 1], ALU.add).then_inc(gcut, 1)
                    for t in range(NT):
                        ins = dve.max_index(topi[:, t, :], top[:, t, :], lg[:, t, :])
                    ins.then_inc(gcut, 1)
                    for e in range(EX):
                        ins = dve.memset(number[:, :, e:e + 1], float(e))
                    ins.then_inc(gcut, 1)
                    dve.wait_ge(gcut, 10)
                    dve.tensor_scalar(small[:, 0, :], small[:, 0, :], 1e-20, None, ALU.add).then_inc(gcut, 1)
                    dve.tensor_copy(topf[:, :, :], topi[:, :, 0:2]).then_inc(gcut, 1)
                    dve.wait_ge(gcut, 12)
                    dve.reciprocal(small[:, 1, :], small[:, 0, :]).then_inc(gcut, 1)
                    for m in range(2):
                        dve.tensor_tensor(chosen[:, m, :, :], number[:, :, :], wide(topf[:, :, m]),
                                          ALU.is_equal).then_inc(gcut, 1)
                    dve.wait_ge(gcut, 15)
                    dve.tensor_tensor(chosen[:, 0, :, :], chosen[:, 0, :, :], chosen[:, 1, :, :], ALU.add).then_inc(gcut, 1)
                    dve.wait_ge(gcut, 16)
                    dve.tensor_tensor(lg[:, :, :], lg[:, :, :], chosen[:, 0, :, :], ALU.mult).then_inc(gcut, 1)
                    dve.wait_ge(gcut, 17)
                    dve.tensor_tensor(cw[:, :, 0:EX], lg[:, :, :], wide(small[:, 1, :]), ALU.mult).then_inc(gcut, 1)
                    dve.wait_ge(gcut, 18)
                for e in range(E):
                    dve.wait_ge(whi_ok, e + 1)
                    dve.tensor_tensor(w1lo[:, e, :, :], st1[:, e % 2, :, :], f(w1hi[:, e, :, :]), ALU.subtract)
                    dve.tensor_tensor(w2lo[:, e, :, :], st2[:, e % 2, :, :], f(w2hi[:, e, :, :]),
                                      ALU.subtract).then_inc(wlo_ok, 1)
                if rest:
                    dve.wait_ge(zeroed, 2)

                def add(j, k):
                    n, e = 2 * E * j + k, k % E
                    dve.wait_ge(y_full, cnth(n))
                    if gate_w is None:
                        tok = bass.ds(2 * TPC * j + TPC * (k // E), TPC)
                        ins = dve.tensor_tensor(X[:, tok, :], py[:, :, :], X[:, tok, :], ALU.add)
                    else:
                        for t in range(TPC):
                            tok = bass.ds(2 * TPC * j + (TPC * (k // E) + t), 1)
                            x = X[:, tok, :].rearrange("p o d -> p (o d)")
                            ins = dve.scalar_tensor_tensor(out=x, in0=py[:, t, :], scalar=cw[:, tok, e],
                                                           in1=x, op0=ALU.mult, op1=ALU.add)
                    ins.then_inc(y_out, 1)

                dve.sem_inc(h_ok, CREDIT)
                dve.sem_inc(y_out, 1)
                with dve.Fori(0, NCH // 2) as j:
                    for k in range(2 * E):
                        n, h = 2 * E * j + k, k % 2
                        dve.wait_ge(sg_ok, nth(n))
                        ins = dve.tensor_tensor(hf[:, h, 0, :], sg[:, h, 0, :], pg[h][:, 1, :], ALU.mult)
                        if rest:
                            ins = dve.tensor_tensor(hf[0:48, h, 1, :], sg[UO:UO + 48, h, 1, :], pg[h][UO:UO + 48, 2, :],
                                                    ALU.mult)
                        ins.then_inc(h_ok, 1)
                        dve.wait_ge(hi_ok, nth(n))
                        ins = dve.tensor_tensor(hlo[:, h, 0, :], hf[:, h, 0, :], f(hhi[:, h, 0, :]), ALU.subtract)
                        if rest:
                            ins = dve.tensor_tensor(hlo[0:48, h, 1, :], hf[0:48, h, 1, :], f(hhi[0:48, h, 1, :]),
                                                    ALU.subtract)
                        ins.then_inc(lo_ok, 1)
                        if k >= 1:
                            add(j, k - 1)
                    add(j, 2 * E - 1)


def hadamard_down(nc, name, ident, w2t, scr):
    NB = w2t.shape[0] // P
    with Phase(nc, name) as ph:
        w = [ph.sb(f"w{u}", [P, NB, D]) for u in range(2)]
        h = [ph.sb(f"h{u}", [P, P]) for u in range(2)]
        out = ph.sb("out", [P, NB, D])
        acc = ph.psum("acc", [P, NB, D])
        loaded, step, mul, scaled, stored = (ph.sem(n) for n in ("loaded", "step", "mul", "scaled", "stored"))
        with nc.Block() as block:
            @block.sync
            def _(sp):
                sp.dma_start(w[0][:, :, :], w2t.rearrange("(k p) n -> p k n", p=P)).then_inc(loaded, 16)
                sp.wait_ge(scaled, 1)
                sp.dma_start(scr.rearrange("k o p n -> p (k o) n"), out[:, :, :]).then_inc(stored, 16)
                sp.wait_ge(stored, 16)

            @block.vector
            def _(dve):
                done, at = 0, 0
                dve.tensor_copy(h[0][:, :], ident[:, :]).then_inc(step, 1)
                done += 1
                g = 1
                while g < P:
                    dve.wait_ge(step, done)
                    a = h[at][:, :].rearrange("p (m two g) -> p m two g", two=2, g=g)
                    c = h[1 - at][:, :].rearrange("p (m two g) -> p m two g", two=2, g=g)
                    dve.tensor_tensor(c[:, :, 0, :], a[:, :, 0, :], a[:, :, 1, :], ALU.add).then_inc(step, 1)
                    dve.tensor_tensor(c[:, :, 1, :], a[:, :, 0, :], a[:, :, 1, :], ALU.subtract).then_inc(step, 1)
                    done, at, g = done + 2, 1 - at, 2 * g
                dve.wait_ge(loaded, 16)
                g, bt = 1, 0
                while g < NB:
                    dve.wait_ge(step, done)
                    a = w[bt][:, :, :].rearrange("p (m two g) n -> p m two (g n)", two=2, g=g)
                    c = w[1 - bt][:, :, :].rearrange("p (m two g) n -> p m two (g n)", two=2, g=g)
                    dve.tensor_tensor(c[:, :, 0, :], a[:, :, 0, :], a[:, :, 1, :], ALU.add).then_inc(step, 1)
                    dve.tensor_tensor(c[:, :, 1, :], a[:, :, 0, :], a[:, :, 1, :], ALU.subtract).then_inc(step, 1)
                    done, bt, g = done + 2, 1 - bt, 2 * g

            @block.tensor
            def _(pe):
                pe.wait_ge(step, 1 + 2 * 7 + 2 * 3)
                for q in range(NB // 2):
                    ins = pe.matmul(acc[:, 2 * q:2 * q + 2, :], h[1][:, :], w[1][:, 2 * q:2 * q + 2, :],
                                    start=True, stop=True)
                ins.then_inc(mul, 1)

            @block.scalar
            def _(act):
                act.wait_ge(mul, 1)
                act.activation(out[:, :, :], acc[:, :, :], ACT.Copy, scale=float(NB * P) ** -0.5).then_inc(scaled, 1)


def wide_attention(nc, name, X, xn, ident, w_qkv, b_qk, b_v, w_out, b_out):
    xhi, xlo = xn
    scale = float(D) ** -0.5
    NHALF = S // CH
    with Phase(nc, name) as ph:
        stage = ph.sb("stage", [P, KT, 3 * D])
        ostage = ph.sb("ostage", [P, KT, D])
        whi, wlo = ph.sb("whi", [P, KT, 3 * D], F32R), ph.sb("wlo", [P, KT, 3 * D], F32R)
        ohi, olo = ph.sb("ohi", [P, KT, D], F32R), ph.sb("olo", [P, KT, D], F32R)
        bias = ph.sb("bias", [P, 4])
        vb, ob = ph.sb("vb", [P, D]), ph.sb("ob", [P, D])
        qkhi, qklo = ph.sb("qkhi", [P, 2, KT, S], F32R), ph.sb("qklo", [P, 2, KT, S], F32R)
        vhi, vlo = ph.sb("vhi", [P, ST, D], F32R), ph.sb("vlo", [P, ST, D], F32R)
        vx = ph.sb("vx", [P, 2, 2, KT, P], F32R)
        vf = ph.sb("vf", [P, 2, D])
        pr = ph.sb("pr", [P, 2, S])
        neg = ph.sb("neg", [P, 2, 2])
        sums, inv = ph.sb("sums", [P, 2, TPC]), ph.sb("inv", [P, 2, TPC])
        pthi, ptlo = ph.sb("pthi", [P, ST, CH], F32R), ph.sb("ptlo", [P, ST, CH], F32R)
        chi, clo = ph.sb("chi", [P, KT, CH], F32R), ph.sb("clo", [P, KT, CH], F32R)
        work = ph.psum("work", [P, 2, CH])
        sc = ph.psum("sc", [P, 2, S])
        turned = ph.psum("turned", [P, ST, P])
        loaded, whi_ok, wlo_ok, based = (ph.sem(n) for n in ("loaded", "whi_ok", "wlo_ok", "based"))
        work_full, work_free, vcopy, own = (ph.sem(n) for n in ("work_full", "work_free", "vcopy", "own"))
        sc_full, max_ok, exp_ok, turn_full, pt_hi, pt_lo, c_ok = (
            ph.sem(n) for n in ("sc_full", "max_ok", "exp_ok", "turn_full", "pt_hi", "pt_lo", "c_ok"))
        loads = [(stage[:, :, :], w_qkv.rearrange("(k p) n -> p k n", p=P)),
                 (ostage[:, :, :], w_out.rearrange("(k p) n -> p k n", p=P)),
                 (bias[:, :], b_qk[:, 0:2 * KT]),
                 (vb[:, :], b_v.partition_broadcast(P)),
                 (ob[:, :], b_out.partition_broadcast(P))]
        QK = [(w, m, c) for w in range(2) for m in range(KT) for c in range(NHALF)]
        AT_V = len(QK)
        AT_C = [AT_V + ST + half * (KT + TPC) for half in range(NHALF)]
        STEPS = AT_V + ST + NHALF * (KT + TPC)
        OWN = len(QK) + 2 * ST + ST + NHALF * (KT + 1)

        def in_order(scores, turn, half_end):
            scores(0)
            for t in range(1, ST):
                scores(t)
                turn(t - 1)
                if t % TPC == 0:
                    half_end(t // TPC - 1)
            turn(ST - 1)
            half_end(NHALF - 1)

        with nc.Block() as block:
            @block.sync
            def _(sp):
                for dst, src in loads:
                    sp.dma_start(dst, src).then_inc(loaded, 16)

            @block.gpsimd
            def _(pool):
                with pool.Fori(0, B) as b:
                    for t in range(ST):
                        pool.wait_ge(work_full, STEPS * b + (AT_V + t - 1))
                        at = bass.ds(S * b + t * P, P)
                        pool.tensor_copy(vx[:, t % 2, 0, :, :], f(xhi[:, :, at]))
                        pool.tensor_copy(vx[:, t % 2, 1, :, :], f(xlo[:, :, at])).then_inc(vcopy, 1)

            @block.tensor
            def _(pe):
                pe.wait_ge(wlo_ok, 2)
                with pe.Fori(0, B) as b:
                    def step(at, out, pairs):
                        pe.wait_ge(work_free, two_back(STEPS * b + at))
                        three_terms(pe, out, pairs).then_inc(work_full, 1)

                    for n, (w, m, c) in enumerate(QK):
                        cs = slice(w * D + m * P, w * D + (m + 1) * P)
                        at = bass.ds(S * b + c * CH, CH)
                        step(n, work[:, n % 2, :], [((whi[:, k, cs], wlo[:, k, cs]), (xhi[:, k, at], xlo[:, k, at]))
                                                    for k in range(KT)])
                    for t in range(ST):
                        n = AT_V + t
                        pe.wait_ge(vcopy, ST * b + (t + 1))
                        step(n, work[:, n % 2, 0:D],
                             [((vx[:, t % 2, 0, k, :], vx[:, t % 2, 1, k, :]),
                               (whi[:, k, 2 * D:3 * D], wlo[:, k, 2 * D:3 * D])) for k in range(KT)])
                    pe.wait_ge(work_free, cnth(STEPS * b + (AT_V + ST - 1)))

                    def scores(t):
                        g = ST * b + t
                        pe.wait_ge(exp_ok, two_back(g))
                        ts = slice(t * P, (t + 1) * P)
                        for c in range(NHALF):
                            cs = slice(c * CH, (c + 1) * CH)
                            ins = three_terms(pe, sc[:, t % 2, cs],
                                              [((qkhi[:, 0, k, ts], qklo[:, 0, k, ts]),
                                                (qkhi[:, 1, k, cs], qklo[:, 1, k, cs])) for k in range(KT)])
                        ins.then_inc(sc_full, 1)

                    def turn(t):
                        g = ST * b + t
                        pe.wait_ge(exp_ok, cnth(g))
                        pe.wait_ge(pt_lo, g + 1)
                        for k in range(ST):
                            ins = pe.transpose(turned[:, k, :], pr[:, t % 2, k * P:(k + 1) * P], ident[:, :])
                        ins.then_inc(turn_full, 1)

                    def half_end(half):
                        pe.wait_ge(pt_lo, ST * b + (TPC * (half + 1) + 1))
                        for m in range(KT):
                            n = AT_C[half] + m
                            ms = slice(m * P, (m + 1) * P)
                            step(n, work[:, n % 2, :], [((vhi[:, k, ms], vlo[:, k, ms]), (pthi[:, k, :], ptlo[:, k, :]))
                                                        for k in range(ST)])
                        pe.wait_ge(c_ok, NHALF * b + (half + 1))
                        for t in range(TPC):
                            n = AT_C[half] + KT + t
                            ts = slice(t * P, (t + 1) * P)
                            step(n, work[:, n % 2, 0:D], [((chi[:, k, ts], clo[:, k, ts]), (ohi[:, k, :], olo[:, k, :]))
                                                          for k in range(KT)])

                    in_order(scores, turn, half_end)

            @block.scalar
            def _(act):
                act.sem_inc(exp_ok, CREDIT)
                act.wait_ge(loaded, 16 * len(loads))
                act.activation(whi[:, :, :], stage[:, :, :], ACT.Copy).then_inc(whi_ok, 1)
                act.activation(ohi[:, :, :], ostage[:, :, :], ACT.Copy).then_inc(whi_ok, 1)
                with act.Fori(0, B) as b:
                    def scores(t):
                        g = ST * b + t
                        act.wait_ge(max_ok, nth(g))
                        act.wait_ge(turn_full, two_back(g))
                        act.activation(pr[:, t % 2, :], sc[:, t % 2, :], ACT.Exp, bias=neg[:, t % 2, 1:2], scale=scale,
                                       accum_out=sums[:, t // TPC, t % TPC:t % TPC + 1]).then_inc(exp_ok, 1)

                    def turn(t):
                        act.wait_ge(turn_full, cnth(ST * b + t))
                        if t == TPC:
                            act.wait_ge(work_full, STEPS * b + (AT_C[0] + KT))
                        cs = slice(t % TPC * P, (t % TPC + 1) * P)
                        act.activation(pthi[:, :, cs], turned[:, :, :], ACT.Copy).then_inc(pt_hi, 1)

                    in_order(scores, turn, lambda half: None)

            @block.vector
            def _(dve):
                dve.sem_inc(work_free, CREDIT)
                dve.sem_inc(pt_lo, 1)
                dve.sem_inc(turn_full, CREDIT)
                dve.wait_ge(whi_ok, 1)
                dve.tensor_tensor(wlo[:, :, :], stage[:, :, :], f(whi[:, :, :]), ALU.subtract).then_inc(wlo_ok, 1)
                dve.wait_ge(whi_ok, 2)
                dve.tensor_tensor(olo[:, :, :], ostage[:, :, :], f(ohi[:, :, :]), ALU.subtract).then_inc(wlo_ok, 1)
                for t in range(NT):
                    ins = dve.tensor_tensor(X[:, t, :], X[:, t, :], ob[:, :], ALU.add)
                ins.then_inc(based, 1)
                dve.wait_ge(based, 1)
                with dve.Fori(0, B) as b:
                    count = [0]

                    def chain(ins):
                        ins.then_inc(own, 1)
                        count[0] += 1
                        dve.wait_ge(own, OWN * b + count[0])

                    for n, (w, m, c) in enumerate(QK):
                        col = bias[:, w * KT + m:w * KT + m + 1]
                        hi, lo = (t[:, w, m, c * CH:(c + 1) * CH] for t in (qkhi, qklo))
                        dve.wait_ge(work_full, STEPS * b + (n + 1))
                        chain(dve.tensor_scalar(hi, work[:, n % 2, :], col, None, ALU.add))
                        dve.scalar_tensor_tensor(out=lo, in0=work[:, n % 2, :], scalar=col, in1=f(hi),
                                                 op0=ALU.add, op1=ALU.subtract).then_inc(work_free, 1)
                    for t in range(ST):
                        n = AT_V + t
                        dve.wait_ge(work_full, STEPS * b + (n + 1))
                        chain(dve.tensor_tensor(vf[:, t % 2, :], work[:, n % 2, 0:D], vb[:, :], ALU.add))
                        chain(dve.tensor_copy(vhi[:, t, :], vf[:, t % 2, :]))
                        dve.tensor_tensor(vlo[:, t, :], vf[:, t % 2, :], f(vhi[:, t, :]),
                                          ALU.subtract).then_inc(work_free, 1)

                    def scores(t):
                        dve.wait_ge(sc_full, ST * b + (t + 1))
                        chain(dve.tensor_reduce(neg[:, t % 2, 0:1], sc[:, t % 2, :], AX.X, ALU.max, negate=True))
                        dve.tensor_scalar(neg[:, t % 2, 1:2], neg[:, t % 2, 0:1], scale, None, ALU.mult).then_inc(max_ok, 1)

                    def turn(t):
                        dve.wait_ge(pt_hi, ST * b + (t + 1))
                        cs = slice(t % TPC * P, (t % TPC + 1) * P)
                        dve.tensor_tensor(ptlo[:, :, cs], turned[:, :, :], f(pthi[:, :, cs]),
                                          ALU.subtract).then_inc(pt_lo, 1)

                    def half_end(half):
                        for m in range(KT):
                            n = AT_C[half] + m
                            dve.wait_ge(work_full, STEPS * b + (n + 1))
                            chain(dve.tensor_copy(chi[:, m, :], work[:, n % 2, :]))
                            ins = dve.tensor_tensor(clo[:, m, :], work[:, n % 2, :], f(chi[:, m, :]), ALU.subtract)
                            ins.then_inc(work_free, 1)
                        dve.wait_ge(work_free, cnth(STEPS * b + (AT_C[half] + KT - 1)))
                        dve.wait_ge(exp_ok, cnth(ST * b + (TPC * (half + 1) - 1)))
                        chain(dve.reciprocal(inv[:, half, :], sums[:, half, :]))
                        dve.sem_inc(c_ok, 1)
                        for t in range(TPC):
                            n = AT_C[half] + KT + t
                            dve.wait_ge(work_full, STEPS * b + (n + 1))
                            x = X[:, bass.ds(ST * b + half * TPC + t, 1), :].rearrange("p o d -> p (o d)")
                            dve.scalar_tensor_tensor(out=x, in0=work[:, n % 2, 0:D], scalar=inv[:, half, t:t + 1],
                                                     in1=x, op0=ALU.mult, op1=ALU.add).then_inc(work_free, 1)

                    in_order(scores, turn, half_end)
                    assert count[0] == OWN


def store(nc, X, out):
    with Phase(nc, "store") as ph:
        stored = ph.sem("stored")
        with nc.Block() as block:
            @block.sync
            def _(sp):
                sp.dma_start(out.rearrange("b (n p) d -> p (b n) d", p=P), X[:, :, :]).then_inc(stored, 16)
                sp.wait_ge(stored, 16)


def build(nc, i, out, stop=None):
    def scratch(name, shape):
        return nc.dram_tensor(name, shape, F32, kind="Internal").ap()

    with ExitStack() as ctx:
        def sb(name, shape, dt=F32):
            return ctx.enter_context(nc.sbuf_tensor(name, shape, dt))

        X = sb("X", [P, NT, D])
        ident = sb("ident", [P, P])
        ident_bf, mask_qk, mask_kq = sb("ident_bf", [P, P], BF16), sb("mask_qk", [P, P], BF16), sb("mask_kq", [P, P], BF16)
        q16, k16 = scratch("q16", [2, 8, 4, 16, S]), scratch("k16", [2, 8, 4, 16, S])
        q8, k8 = scratch("q8", [2, 16, 4, 8, S]), scratch("k8", [2, 16, 1, 8, S])
        down = scratch("down", [8, 1, P, D])

        def channels(name):
            stack = ExitStack()
            return stack, [stack.enter_context(nc.sbuf_tensor(f"{name}_x{n}", [P, KT, T], F32R)) for n in ("hi", "lo")]

        def heads(name, norm, project, dh, q, k, scale, causal, w_out, b_out):
            with nc.sbuf_tensor(f"{name}_V", [P, q.shape[1], ST, k.shape[2] * dh], F32) as V:
                stack, xn = channels(name)
                with stack:
                    norm(xn)
                    project(xn, V)
                with nc.sbuf_tensor(f"{name}_O", [P, ST, q.shape[1], 4 * dh], F32) as O:
                    attention(nc, f"{name}_at", q, k, V, O, ident, ident_bf, mask_qk, mask_kq, dh, scale, causal)
                    out_projection(nc, f"{name}_out", X, O, ident, w_out, b_out)

        def ffn(name, w1, w2, rest, gate_w=None):
            stack, xn = channels(name)
            with stack:
                normed(nc, f"{name}_n", X, ident, xn)
                gated_ffn(nc, name, X, xn, ident, w1, w2, rest, gate_w)

        def layer0():
            yield lambda: heads(
                "a0", lambda xn: normed(nc, "a0_n", X, ident, xn, RMS_EPS),
                lambda xn, V: qkv(nc, "a0_p", ident, xn,
                                  [(0, D, i["L0_attn_a_Wq"]), (D, 3 * D, i["L0_attn_a_Wkv"])], 16, q16, k16, P, V, D,
                                  in_gain=(i["cols_L0_attn_a_g_q"], i["cols_L0_attn_a_g_kv"]),
                                  q_bias=i["cols_L0_attn_a_bq"], k_bias=i["cols_L0_attn_a_bkv"], v_bias=i["L0_attn_a_bkv"][D:2 * D],
                                  head_gain=i["L0_attn_a_g_head"]),
                16, q16, k16, 16 ** -0.5, False, i["L0_attn_a_Wo"], i["L0_attn_a_bo"])
            yield lambda: ffn("m0", i["moe_w1"], i["moe_w2"], True, i["moe_gate"])

            def wide():
                stack, xn = channels("b0")
                with stack:
                    normed(nc, "b0_n", X, ident, xn)
                    wide_attention(nc, "b0", X, xn, ident, i["wide_qkv"], i["cols_L0_attn_b_b_qkv"],
                                   i["L0_attn_b_b_qkv"][2 * D:3 * D], i["wide_out"],
                                   i["L0_attn_b_b_out"])
            yield wide
            yield lambda: ffn("m1", i["moe_w1"], i["moe_w2"], True, i["moe_gate"])

        def layer1():
            yield lambda: hadamard_down(nc, "had", ident, i["ffn_w2"], down)
            yield lambda: heads(
                "a1", lambda xn: normed(nc, "a1_n", X, ident, xn, LN_EPS, i["cols_L1_attn_a_ln_g"],
                                  i["cols_L1_attn_a_ln_b"]),
                lambda xn, V: qkv(nc, "a1_p", ident, xn,
                                  [(n * D, (n + 1) * D, i[f"L1_attn_a_W{w}"]) for n, w in enumerate("qkv")],
                                  16, q16, k16, P, V, D, q_bias=i["cols_L1_attn_a_bq"], k_bias=i["cols_L1_attn_a_bk"],
                                  v_bias=i["L1_attn_a_bv"]),
                16, q16, k16, 16 ** -0.5, True, i["L1_attn_a_Wo"], i["L1_attn_a_bo"])
            yield lambda: ffn("f0", i["ffn_w1"], down, False)
            yield lambda: heads(
                "b1", lambda xn: normed(nc, "b1_n", X, ident, xn),
                lambda xn, V: qkv(nc, "b1_p", ident, xn,
                                  [(0, D, i["L1_attn_b_Wq"]), (D, D + 64, i["L1_attn_b_Wk"]),
                                   (D + 64, D + 128, i["L1_attn_b_Wv"])], 8, q8, k8, 64, V, 64),
                8, q8, k8, 8 ** -0.5, True, i["L1_attn_b_Wo"], None)
            yield lambda: ffn("f1", i["ffn_w1"], down, False)

        setup(nc, i["L0_attn_a_x"], X, ident, ident_bf, mask_qk, mask_kq)
        for n, phase in enumerate([*layer0(), *layer1()]):
            if stop is None or n in stop:
                phase()
        store(nc, X, out)


_DIRECT = ["L0_attn_a_x", "L0_attn_a_Wq", "L0_attn_a_Wkv", "L0_attn_a_bkv", "L0_attn_a_g_head", "L0_attn_a_Wo",
           "L0_attn_a_bo", "L0_attn_b_b_qkv", "L0_attn_b_b_out", "L1_attn_a_Wq", "L1_attn_a_Wk", "L1_attn_a_Wv",
           "L1_attn_a_bv", "L1_attn_a_Wo", "L1_attn_a_bo", "L1_attn_b_Wq", "L1_attn_b_Wk", "L1_attn_b_Wv",
           "L1_attn_b_Wo"]


_COLUMNS = ["L0_attn_a_g_q", "L0_attn_a_g_kv", "L0_attn_a_bq", "L0_attn_a_bkv", "L0_attn_b_b_qkv",
            "L1_attn_a_ln_g", "L1_attn_a_ln_b", "L1_attn_a_bq", "L1_attn_a_bk"]


def lay_out(inputs):
    import numpy as np

    a = {n: np.asarray(v) for n, v in inputs.items()}
    out = {n: a[n] for n in _DIRECT}
    out |= {f"cols_{n}": a[n].reshape(-1, 128).T for n in _COLUMNS}
    w1, w2 = a["L0_ffn_w1"], a["L0_ffn_w2"]
    E, D_, I2 = w1.shape
    I = I2 // 2
    moe1 = np.zeros((E + 1, D_, 3 * 128 - 16), w1.dtype)
    moe2 = np.zeros((E + 1, 2, 128, D_), w1.dtype)
    for e in range(E + 1):
        g, u = (w1[e, :, :I], w1[e, :, I:]) if e < E else (a["L0_ffn_sw1"].T, a["L0_ffn_sw2"].T)
        d = w2[e] if e < E else a["L0_ffn_sw3"].T
        moe1[e, :, 0:128], moe1[e, :, 128:256] = g[:, :128], u[:, :128]
        moe1[e, :, 256:256 + I - 128], moe1[e, :, 320:320 + I - 128] = g[:, 128:], u[:, 128:]
        moe2[e, 0], moe2[e, 1, :I - 128] = d[:128], d[128:]
    out["moe_w1"], out["moe_w2"], out["moe_gate"] = moe1, moe2, a["L0_ffn_gate_w"].T
    out["wide_qkv"], out["wide_out"] = a["L0_attn_b_w_qkv"].T, a["L0_attn_b_w_out"].T
    W1, W3 = a["L1_ffn_W1"].T, a["L1_ffn_W3"].T
    blocks = [np.concatenate([W1[:, n:n + 128], W3[:, n:n + 128]], axis=1) for n in range(0, W1.shape[1], 128)]
    out["ffn_w1"], out["ffn_w2"] = np.stack(blocks), a["L1_ffn_W2"].T
    return {n: np.ascontiguousarray(v) for n, v in out.items()}


def kernel(**inputs):
    import concourse.bacc as bacc
    from concourse.bass_utils import run_bass_kernel_spmd

    nc = bacc.Bacc("TRN2", target_bir_lowering=False, num_devices=1)
    arrays = {f"in_{n}": v for n, v in lay_out(inputs).items()}
    aps = {n[3:]: nc.dram_tensor(n, v.shape, mybir.dt.from_np(v.dtype), kind="ExternalInput").ap()
           for n, v in arrays.items()}
    out = nc.dram_tensor("out", inputs["L0_attn_a_x"].shape, F32, kind="ExternalOutput").ap()
    build(nc, aps, out)
    r = run_bass_kernel_spmd(nc, [arrays], core_ids=[0])
    return r.results[0]["out"]
```

```python
from contextlib import ExitStack

import concourse.bass as bass
from concourse import mybir

F32 = mybir.dt.float32
F32R = mybir.dt.float32r
BF16 = mybir.dt.bfloat16
ACT = mybir.ActivationFunctionType
ALU = mybir.AluOpType
AX = mybir.AxisListType

P = 128
D = 256
KT = D // P
B, S = 2, 1024
T = B * S
NT = T // P
CH = 512
NCH = T // CH
TPC = CH // P
ST = S // P
ROWS = 96
NEG = -1e30
LN_EPS = 1e-5
RMS_EPS = 1.1920928955078125e-07


class Phase:

    def __init__(self, nc, name):
        self.nc, self.name, self.stack, self.sems = nc, name, ExitStack(), []

    def __enter__(self):
        self.stack.__enter__()
        return self

    def sb(self, name, shape, dt=F32):
        return self.stack.enter_context(self.nc.sbuf_tensor(f"{self.name}_{name}", shape, dt))

    def psum(self, name, shape, dt=F32):
        return self.stack.enter_context(self.nc.psum_tensor(f"{self.name}_{name}", shape, dt))

    def sem(self, name):
        s = self.nc.alloc_semaphore(f"{self.name}_{name}")
        self.sems.append(s)
        return s

    def __exit__(self, *exc):
        if exc[0] is None:
            self.nc.clear_and_free_semaphores(self.sems)
            self.nc.all_engine_barrier()
        return self.stack.__exit__(*exc)


class Weight:

    def __init__(self, nc, stack, short, name, pieces, gains=None):
        self.pieces, self.gains = pieces, gains
        width = max(b for _, b, _ in pieces)

        def sb(where, part, shape, dt=F32):
            return where.enter_context(nc.sbuf_tensor(f"{name}_{part}", shape, dt))

        self.hi, self.lo = (sb(stack, part, [P, KT, width], F32R) for part in ("hi", "lo"))
        self.stage = sb(short, "stage", [P, KT, width])
        if gains is not None:
            self.gain = sb(short, "gain", [P, len(gains), KT])

    def loads(self):
        out = [(self.stage[:, :, a:b], w.rearrange("(k p) n -> p k n", p=P)) for a, b, w in self.pieces]
        if self.gains is not None:
            out += [(self.gain[:, n, :], g) for n, g in enumerate(self.gains)]
        return out


class Preparation:

    def __init__(self, ph, weights):
        self.weights = weights
        if weights:
            self.arrived, self.cut = ph.sem("weights_arrived"), ph.sem("weights_cut")

    def load(self, sp):
        for w in self.weights:
            for dst, src in w.loads():
                sp.dma_start(dst, src).then_inc(self.arrived, 16)

    def cut_all(self, pool):
        done = 0
        if self.weights:
            pool.wait_ge(self.arrived, 16 * sum(len(w.loads()) for w in self.weights))
        for w in self.weights:
            if w.gains is not None:
                for n, (a, b, _) in enumerate(w.pieces):
                    for k in range(KT):
                        gain = w.gain[:, n, k:k + 1].broadcast_to([P, b - a])
                        part = w.stage[:, k, a:b]
                        pool.tensor_tensor(part, part, gain, ALU.mult).then_inc(self.cut, 1)
                done += len(w.pieces) * KT
                pool.wait_ge(self.cut, done)
            pool.tensor_copy(w.hi[:, :, :], w.stage[:, :, :]).then_inc(self.cut, 1)
            pool.wait_ge(self.cut, done + 1)
            pool.tensor_tensor(w.lo[:, :, :], w.stage[:, :, :], f(w.hi[:, :, :]), ALU.subtract).then_inc(self.cut, 1)
            done += 2


class Experts:

    def __init__(self, nc, stack, name, w1, w2, gate=None):
        self.w1, self.w2, self.gate = w1, w2, gate
        self.ahead = 2 if gate is not None else 3
        E, W1, K2 = w1.shape[0], w1.shape[2], w2.shape[1]

        def sb(part, shape, dt=F32):
            return stack.enter_context(nc.sbuf_tensor(f"{name}_{part}", shape, dt))

        self.w1hi, self.w1lo = sb("w1hi", [P, E, KT, W1], F32R), sb("w1lo", [P, E, KT, W1], F32R)
        self.w2hi, self.w2lo = sb("w2hi", [P, E, K2, D], F32R), sb("w2lo", [P, E, K2, D], F32R)
        self.st1, self.st2 = sb("st1", [P, 2, KT, W1]), sb("st2", [P, 2, K2, D])
        if gate is not None:
            self.gst = sb("gst", [P, KT, E - 1])
            self.ghi, self.glo = sb("ghi", [P, KT, P], F32R), sb("glo", [P, KT, P], F32R)

    def semaphores(self, ph):
        self.loaded = [ph.sem(f"expert_loaded{u}") for u in range(2)]
        self.hi_cut, self.lo_cut, self.gate_in, self.gate_cut = (
            ph.sem(n) for n in ("expert_hi", "expert_lo", "gate_in", "gate_cut"))

    def load_gate(self, sp):
        if self.gate is not None:
            sp.dma_start(self.gst[:, :, :], self.gate.rearrange("(k p) e -> p k e", p=P)).then_inc(self.gate_in, 16)

    def load(self, sp, first, end):
        for n, e in enumerate(range(first, end)):
            if n >= 2:
                sp.wait_ge(self.lo_cut, n - 1)
            for dst, src in ((self.st1[:, n % 2, :, :], self.w1[e].rearrange("(k p) n -> p k n", p=P)),
                             (self.st2[:, n % 2, :, :], self.w2[e].rearrange("k p n -> p k n"))):
                sp.dma_start(dst, src).then_inc(self.loaded[n % 2], 16)

    def cut_gate(self, pool):
        if self.gate is not None:
            for n, t in enumerate((self.ghi, self.glo)):
                pool.memset(t[:, :, :].bitcast(F32), 0.0).then_inc(self.gate_cut, 1)
            pool.wait_ge(self.gate_cut, 2)
            pool.wait_ge(self.gate_in, 16)
            columns = slice(0, self.gst.shape[2])
            pool.tensor_copy(self.ghi[:, :, columns], self.gst[:, :, :]).then_inc(self.gate_cut, 1)
            pool.wait_ge(self.gate_cut, 3)
            pool.tensor_tensor(self.glo[:, :, columns], self.gst[:, :, :], f(self.ghi[:, :, columns]),
                               ALU.subtract).then_inc(self.gate_cut, 1)

    def cut(self, pool, first, end):
        for n, e in enumerate(range(first, end)):
            u = n % 2
            pool.wait_ge(self.loaded[u], 32 * (n // 2 + 1))
            pool.tensor_copy(self.w1hi[:, e, :, :], self.st1[:, u, :, :])
            pool.tensor_copy(self.w2hi[:, e, :, :], self.st2[:, u, :, :]).then_inc(self.hi_cut, 1)
            pool.wait_ge(self.hi_cut, n + 1)
            pool.tensor_tensor(self.w1lo[:, e, :, :], self.st1[:, u, :, :], f(self.w1hi[:, e, :, :]), ALU.subtract)
            pool.tensor_tensor(self.w2lo[:, e, :, :], self.st2[:, u, :, :], f(self.w2hi[:, e, :, :]),
                               ALU.subtract).then_inc(self.lo_cut, 1)


CREDIT = 2


def nth(n):
    return n + 1


def cnth(n):
    return n + (1 + CREDIT)


def two_back(n):
    return n + (CREDIT - 1)


def f(ap):
    return ap.bitcast(F32)


def three_terms(pe, out, pairs, start=True, stop=True):
    last = None
    for n, ((ah, al), (bh, bl)) in enumerate(pairs):
        for m, (a, b) in enumerate(((ah, bh), (al, bh), (ah, bl))):
            last = pe.matmul(out, a, b, start=start and n == 0 and m == 0,
                             stop=stop and n == len(pairs) - 1 and m == 2)
    return last


def setup(nc, ident, masks):
    with Phase(nc, "setup") as ph:
        zeroed, built = ph.sem("zeroed"), ph.sem("built")
        with nc.Block() as block:
            @block.gpsimd
            def _(pool):
                for t in (ident, *masks):
                    pool.memset(t[:, :], 0.0).then_inc(zeroed, 1)
                pool.wait_ge(zeroed, 3)
                pool.affine_select(out=ident[:, :], in_=ident[:, :], compare_op=ALU.not_equal, fill=1.0, base=0,
                                   pattern=[[-1, P]], channel_multiplier=1).then_inc(built, 1)
                for mask, sign in zip(masks, (1, -1)):
                    pool.affine_select(out=mask[:, :], in_=mask[:, :], compare_op=ALU.is_ge, fill=NEG, base=0,
                                       pattern=[[-sign, P]], channel_multiplier=sign).then_inc(built, 1)


def normed(nc, name, X, ident, xn, second_eps=None, gain=None, shift=None, weights=(), experts=None):
    xhi, xlo = xn
    GROUPS = [(0, 1), (1, NCH)]
    with Phase(nc, name) as ph:
        stats = ph.sb("stats", [P, NT, 6])
        mv = ph.sb("mv", [P, NT, 2])
        var_eps = ph.sb("var_eps", [P, 2, NT])
        root = ph.sb("root", [P, 2, NT])
        rstd = ph.sb("rstd", [P, NT])
        rstd2 = ph.sb("rstd2", [P, NT])
        shifts = ph.sb("shifts", [P, NT])
        xt = ph.sb("xt", [P, NT, D])
        cols = ph.sb("cols", [P, 2, KT])
        full = ph.sb("full", [P, 2, KT, CH])
        turned = [ph.psum(f"turned{u}", [P, KT, CH]) for u in range(2)]
        loaded, step, rooted, scales = ph.sem("loaded"), ph.sem("step"), ph.sem("rooted"), ph.sem("scales")
        scaled = ph.sem("scaled_even"), ph.sem("scaled_odd")
        turn, hi_out, lo_out, fulls = (ph.sem(n) for n in ("turn", "hi_out", "lo_out", "fulls"))
        affine = gain is not None
        double = second_eps is not None
        preparation = Preparation(ph, weights)
        if experts is not None:
            experts.semaphores(ph)
        with nc.Block() as block:
            @block.sync
            def _(sp):
                if affine:
                    for n, v in enumerate((gain, shift)):
                        sp.dma_start(cols[:, n, :], v).then_inc(loaded, 16)
                preparation.load(sp)
                if experts is not None:
                    experts.load_gate(sp)
                    experts.load(sp, 0, experts.ahead)

            @block.gpsimd
            def _(pool):
                preparation.cut_all(pool)
                if experts is not None:
                    experts.cut_gate(pool)
                    experts.cut(pool, 0, experts.ahead)

            @block.vector
            def _(dve):
                count = [0]

                def chain(ins):
                    ins.then_inc(step, 1)
                    count[0] += 1
                    dve.wait_ge(step, count[0])

                def lows(c):
                    at = slice(c * CH, (c + 1) * CH)
                    if affine:
                        dve.wait_ge(fulls, c + 1)
                    dve.wait_ge(hi_out, c + 1)
                    src = full[:, c % 2, :, :] if affine else turned[c % 2][:, :, :]
                    dve.tensor_tensor(xlo[:, :, at], src, f(xhi[:, :, at]), ALU.subtract).then_inc(lo_out, 1)

                for g, (c0, c1) in enumerate(GROUPS):
                    a, b = c0 * TPC, c1 * TPC
                    for t in range(a, b):
                        ins = dve.bn_stats(stats[:, t, :], X[:, t, :])
                    chain(ins)
                    for t in range(a, b):
                        ins = dve.bn_aggr(mv[:, t, :], stats[:, t, :])
                    chain(ins)
                    chain(dve.tensor_scalar(var_eps[:, 0, a:b], mv[:, a:b, 1], LN_EPS, None, ALU.add))
                    dve.wait_ge(rooted, g * (1 + double) + 1)
                    ins = dve.reciprocal(rstd[:, a:b], root[:, 0, a:b])
                    if double:
                        chain(ins)
                        chain(dve.tensor_tensor(rstd2[:, a:b], rstd[:, a:b], rstd[:, a:b], ALU.mult))
                        chain(dve.tensor_tensor(rstd2[:, a:b], rstd2[:, a:b], mv[:, a:b, 1], ALU.mult))
                        chain(dve.tensor_scalar(var_eps[:, 1, a:b], rstd2[:, a:b], second_eps, None, ALU.add))
                        dve.wait_ge(rooted, 2 * g + 2)
                        chain(dve.reciprocal(rstd2[:, a:b], root[:, 1, a:b]))
                        ins = dve.tensor_tensor(rstd[:, a:b], rstd[:, a:b], rstd2[:, a:b], ALU.mult)
                    chain(ins)
                    dve.scalar_tensor_tensor(out=shifts[:, a:b], in0=mv[:, a:b, 0], scalar=-1.0, in1=rstd[:, a:b],
                                             op0=ALU.mult, op1=ALU.mult).then_inc(scales, 1)
                    for n in range(a, b, 2):
                        dve.tensor_scalar(xt[:, n, :], X[:, n, :], mv[:, n, 0:1], rstd[:, n:n + 1], ALU.subtract,
                                          ALU.mult).then_inc(scaled[0], 1)
                for c in range(NCH):
                    lows(c)

            @block.tensor
            def _(pe):
                for c in range(NCH):
                    if c >= 2:
                        pe.wait_ge(lo_out, c - 1)
                    for t in range(TPC):
                        n = c * TPC + t
                        pe.wait_ge(scaled[n % 2], n // 2 + 1)
                        for k in range(KT):
                            ins = pe.transpose(turned[c % 2][:, k, t * P:(t + 1) * P],
                                               xt[:, n, k * P:(k + 1) * P], ident[:, :])
                    ins.then_inc(turn, 1)

            @block.scalar
            def _(act):
                per = 4 + 5 * double

                def roots(g):
                    a, b = (c * TPC for c in GROUPS[g])
                    act.wait_ge(step, per * g + 3)
                    act.activation(root[:, 0, a:b], var_eps[:, 0, a:b], ACT.Sqrt).then_inc(rooted, 1)
                    if double:
                        act.wait_ge(step, per * g + 7)
                        act.activation(root[:, 1, a:b], var_eps[:, 1, a:b], ACT.Sqrt).then_inc(rooted, 1)

                def norms(c):
                    act.wait_ge(scales, 1 if c < GROUPS[0][1] else 2)
                    for n in range(c * TPC + 1, (c + 1) * TPC, 2):
                        act.activation(xt[:, n, :], X[:, n, :], ACT.Identity, bias=shifts[:, n:n + 1],
                                       scale=rstd[:, n:n + 1]).then_inc(scaled[1], 1)

                def highs(c):
                    at = slice(c * CH, (c + 1) * CH)
                    act.wait_ge(turn, c + 1)
                    if affine:
                        if c >= 2:
                            act.wait_ge(lo_out, c - 1)
                        for k in range(KT):
                            ins = act.activation(full[:, c % 2, k, :], turned[c % 2][:, k, :], ACT.Identity,
                                                 bias=cols[:, 1, k:k + 1], scale=cols[:, 0, k:k + 1])
                        ins.then_inc(fulls, 1)
                        act.wait_ge(fulls, c + 1)
                        act.activation(xhi[:, :, at], full[:, c % 2, :, :], ACT.Copy).then_inc(hi_out, 1)
                    else:
                        act.activation(xhi[:, :, at], turned[c % 2][:, :, :], ACT.Copy).then_inc(hi_out, 1)

                if affine:
                    act.wait_ge(loaded, 32)
                roots(0)
                norms(0)
                highs(0)
                roots(1)
                norms(1)
                for c in range(1, NCH):
                    if c + 1 < NCH:
                        norms(c + 1)
                    highs(c)


def set_constant_rows(pool, buffers, done):
    for t, value in zip(buffers, (0.0, 1.0)):
        pool.memset(t[0:ROWS, :, :].bitcast(F32), value).then_inc(done, 1)


def qkv(nc, name, xn, weight, first, dh, q_scr, k_scr, k_rows, V, v_cols,
        q_bias=None, k_bias=None, v_bias=None, head_gain=None):
    xhi, xlo = xn
    whi, wlo = weight.hi, weight.lo
    width = whi.shape[2]
    nm = 4 if k_rows == P else 3
    quads = q_scr.shape[1] // B
    qg = P // (4 * dh)
    with Phase(nc, name) as ph:
        bias = ph.sb("bias", [P, nm])
        vb = ph.sb("vb", [P, v_cols])
        hg = ph.sb("hg", [P, 1])
        eps = ph.sb("eps", [P, 1])
        blocks = ph.sb("blocks", [P, P])
        qf = ph.sb("qf", [P, 2, nm, CH])
        sq = ph.sb("sq", [P, 2, nm, CH])
        qn = ph.sb("qn", [P, 2, nm, CH])
        qhi, qlo = ph.sb("qhi", [P, nm, CH], F32R), ph.sb("qlo", [P, nm, CH], F32R)
        pq = ph.psum("pq", [P, 2, CH])
        pr = ph.psum("pr", [P, nm, CH])
        pv = ph.psum("pv", [P, 2, CH])
        vectors_in, first_set = ph.sem("vectors_in"), ph.sem("first_set")
        projected, biased, squared, summed, logged, inverted, headed, cut_hi, cut_lo = (
            ph.sem(n) for n in ("projected", "biased", "squared", "summed", "logged", "inverted", "headed",
                                "cut_hi", "cut_lo"))
        stored = [ph.sem(f"stored{m}") for m in range(nm)]
        blocked, vmul, vout = (ph.sem(n) for n in ("blocked", "vmul", "vout"))
        rms = head_gain is not None
        others = []
        if q_bias is not None:
            others = [(bias[:, 0:KT], q_bias), (bias[:, KT:2 * KT], k_bias[:, 0:KT]),
                      (vb[:, :], v_bias.partition_broadcast(P))]
        if rms:
            others.append((hg[:, :], head_gain))
        PER = 2 * nm
        with nc.Block() as block:
            @block.sync
            def _(sp):
                for dst, src in others:
                    sp.dma_start(dst, src).then_inc(vectors_in, 16)
                for m in range(nm):
                    sp.sem_inc(stored[m], 32)
                with sp.Fori(0, B) as b:
                    for u in range(2):
                        for m in range(nm):
                            n = u * nm + m
                            sp.wait_ge(cut_lo, PER * b + (PER + n + 1))
                            for part, t in enumerate((qhi, qlo)):
                                cs = slice(u * CH, (u + 1) * CH)
                                if m < 2:
                                    dst = q_scr[part, bass.ds(quads * b + qg * m, qg), :, :, cs]
                                elif k_rows == P:
                                    dst = k_scr[part, bass.ds(quads * b + qg * (m - 2), qg), :, :, cs]
                                else:
                                    dst = k_scr[part, bass.ds(quads * b, quads), :, :, cs]
                                rows = P if m < 2 else k_rows
                                sp.dma_start(dst.rearrange("g h p n -> (g h p) n"),
                                             f(t[0:rows, m, :])).then_inc(stored[m], 16)
                for m in range(nm):
                    sp.wait_ge(stored[m], 32 + 32 * NCH)

            @block.gpsimd
            def _(pool):
                if not rms:
                    set_constant_rows(pool, first, first_set)
                if rms:
                    pool.memset(eps[:, :], RMS_EPS).then_inc(blocked, 1)
                    pool.memset(blocks[:, :], 1.0).then_inc(blocked, 1)
                    view = blocks[:, :].rearrange("p (h e) -> p h e", e=dh)
                    pool.wait_ge(blocked, 2)
                    pool.affine_select(out=view, in_=view, compare_op=ALU.is_ge, fill=0.0, base=0,
                                       pattern=[[-dh, P // dh], [0, dh]], channel_multiplier=1).then_inc(blocked, 1)
                    pool.wait_ge(blocked, 3)
                    pool.affine_select(out=view, in_=view, compare_op=ALU.is_ge, fill=0.0, base=dh - 1,
                                       pattern=[[dh, P // dh], [0, dh]], channel_multiplier=-1).then_inc(blocked, 1)
                    with pool.Fori(0, B) as b:
                        for n in range(PER):
                            u, m = n // nm, n % nm
                            pool.wait_ge(biased, PER * b + (n + 1 + CREDIT))
                            pool.wait_ge(summed, PER * b + (n + 1))
                            pool.tensor_tensor(sq[:, u, m, :], qf[:, u, m, :], qf[:, u, m, :], ALU.mult).then_inc(squared, 1)
                    set_constant_rows(pool, first, first_set)

            @block.tensor
            def _(pe):
                pe.sem_inc(summed, PER)
                for b in range(B):
                    for n in range(PER):
                        u, m = n // nm, n % nm
                        at = slice(b * S + u * CH, b * S + (u + 1) * CH)
                        pe.wait_ge(biased, two_back(PER * b + n))
                        cs = slice(m * P, (m + 1) * P)
                        three_terms(pe, pq[:, n % 2, :],
                                    [((whi[:, k, cs], wlo[:, k, cs]), (xhi[:, k, at], xlo[:, k, at]))
                                     for k in range(KT)]).then_inc(projected, 1)
                    if rms:
                        pe.wait_ge(blocked, 4)
                        for n in range(PER):
                            u, m = n // nm, n % nm
                            if m == 0:
                                pe.wait_ge(logged, 2 * b + (u + 1))
                            pe.wait_ge(squared, nth(PER * b + n))
                            pe.matmul(pr[:, m, :], blocks[:, :], sq[:, u, m, :], start=True, stop=True).then_inc(summed, 1)
                    for n in range(b * ST, (b + 1) * ST):
                        pe.wait_ge(vout, two_back(n))
                        ts = slice(n * P, (n + 1) * P)
                        three_terms(pe, pv[:, n % 2, 0:D],
                                    [((xhi[:, k, ts], xlo[:, k, ts]),
                                      (whi[:, k, width - D:width], wlo[:, k, width - D:width]))
                                     for k in range(KT)]).then_inc(vmul, 1)

            @block.scalar
            def _(act):
                act.sem_inc(biased, CREDIT)
                if rms:
                    act.sem_inc(logged, 1)
                if others:
                    act.wait_ge(vectors_in, 16 * len(others))
                with act.Fori(0, B) as b:
                    for n in range(PER):
                        u, m = n // nm, n % nm
                        act.wait_ge(projected, nth(PER * b + n))
                        act.wait_ge(cut_lo, PER * b + (n + 1))
                        if q_bias is not None:
                            act.activation(qf[:, u, m, :], pq[:, n % 2, :], ACT.Identity,
                                           bias=bias[:, m:m + 1]).then_inc(biased, 1)
                        else:
                            act.activation(qf[:, u, m, :], pq[:, n % 2, :], ACT.Copy).then_inc(biased, 1)
                    if rms:
                        act.wait_ge(blocked, 4)
                        for u in range(2):
                            act.wait_ge(summed, PER * b + (PER + (u + 1) * nm))
                            act.wait_ge(cut_lo, PER * b + (u + 1) * nm)
                            act.activation(qn[:, u, :, :], pr[:, :, :], ACT.Ln, bias=eps[:, :],
                                           scale=1.0 / dh).then_inc(logged, 1)
                            act.wait_ge(logged, 2 * b + (u + 2))
                            act.activation(qn[:, u, :, :], qn[:, u, :, :], ACT.Exp, scale=-0.5).then_inc(inverted, 1)

            @block.vector
            def _(dve):
                dve.sem_inc(cut_lo, PER)
                dve.sem_inc(vout, CREDIT)
                if others:
                    dve.wait_ge(vectors_in, 16 * len(others))

                def cut(b, n):
                    u, m, step = n // nm, n % nm, PER * b + n
                    place = qf[:, u, m, :]
                    dve.wait_ge(stored[m], 32 * (2 * b + u + 1))
                    if rms:
                        dve.wait_ge(inverted, 2 * b + (u + 1))
                        dve.scalar_tensor_tensor(out=place, in0=place, scalar=hg[:, :], in1=qn[:, u, m, :],
                                                 op0=ALU.mult, op1=ALU.mult).then_inc(headed, 1)
                        dve.wait_ge(headed, nth(step))
                    else:
                        dve.wait_ge(biased, cnth(step))
                    dve.tensor_copy(qhi[:, m, :], place).then_inc(cut_hi, 1)
                    dve.wait_ge(cut_hi, nth(step))
                    dve.tensor_tensor(qlo[:, m, :], place, f(qhi[:, m, :]), ALU.subtract).then_inc(cut_lo, 1)

                def value(b, t):
                    n = b * ST + t
                    dve.wait_ge(vmul, nth(n))
                    dst = V[:, b * quads:(b + 1) * quads, t, :]
                    src = pv[:, n % 2, D - v_cols:D].rearrange("p (g c) -> p g c", g=quads)
                    if v_bias is not None:
                        dve.tensor_tensor(dst, src, vb[:, :].rearrange("p (g c) -> p g c", g=quads),
                                          ALU.add).then_inc(vout, 1)
                    else:
                        dve.tensor_copy(dst, src).then_inc(vout, 1)

                for b in range(B):
                    if not rms:
                        for n in range(PER):
                            cut(b, n)
                    for t in range(ST):
                        value(b, t)
                        if rms:
                            cut(b, t)


END_COLUMNS, TURN_AFTER = 12000, 4
PARTS, AT = (1, 0, 1, 1, 1), 1


def attention(nc, name, first, q_scr, k_scr, V, O, ident, masks, dh, scale, causal):
    NQ = q_scr.shape[1]
    kh = k_scr.shape[2]
    if causal:
        units = [(0, 0), (0, 1), (0, 2), (1, 0), (1, 4), (0, 3), (1, 1), (1, 5), (1, 6), (1, 7), (1, 2), (1, 3)]
    else:
        units = [(c, kt) for c in range(2) for kt in range(ST)]
    chunks = [(h, qt, kc) for h in range(4) for qt in range(ST) for kc in range(2)
              if not causal or kc * CH < (qt + 1) * P]
    nu = len(units)
    ends = [max(n for n in range(nu) if units[n][0] == c) for c in range(2)]
    LAG = 2
    n1 = len(chunks) + 1
    G = 5
    mrow = 3 * dh
    R = RING = 3

    def span(c, kt):
        q0 = P * (kt - TPC * c) if causal and kt >= TPC * c else 0
        return q0, min(q0, CH - 2 * P)

    def diagonal(n):
        return causal and units[n][1] >= TPC * units[n][0]

    def width(n):
        _, qt, kc = chunks[n]
        return min(CH, (qt + 1) * P - kc * CH) if causal else CH

    before, parts = [], []
    for c, kt in units:
        cols = CH - span(c, kt)[1]
        step = [cols] * 4
        step.insert(AT + 1, 4 * (CH - span(c, kt)[0]))
        before += step
        parts += [sum(step) * part for part in PARTS]
    gaps = G * nu
    LAST = max(g for g in range(gaps) if sum(before[g:]) >= END_COLUMNS)
    share = [sum(parts[(LAST + 1 + m) % gaps] for m in range(g + 1)) / sum(parts) for g in range(gaps)]
    cost = [width(n) + 64 for n in range(len(chunks))]
    gap_of = [next(g for g, x in enumerate(share) if x + 1e-9 >= (sum(cost[:n]) + cost[n] / 2) / sum(cost))
              + LAST + 1 - gaps for n in range(len(chunks))]
    early = sum(g < 0 for g in gap_of)
    late = len(chunks) - early
    assert early > TURN_AFTER

    def in_gap(g, q, first, second, turn):
        for m in range(len(chunks)):
            if gap_of[m] == g and not is_end(q, 1):
                first(m)
        for m in range(early):
            if gap_of[m] + gaps == g:
                if not is_end(q, 2):
                    second(m)
                if m + 1 == TURN_AFTER and not is_end(q, 1):
                    turn()

    def is_end(q, by):
        return isinstance(q[0], int) and R * q[0] + q[1] + by >= NQ

    with Phase(nc, name) as ph:
        Q = [first[0]] + [ph.sb(f"Q{u}", [P, 4, S], F32R) for u in range(1, R)]
        K = [first[1]] + [ph.sb(f"K{u}", [P, kh, S], F32R) for u in range(1, R)]
        VS = [ph.sb(f"VS{u}", [P, ST, kh, 32]) for u in range(R)]
        mask_qk = masks[0]
        ident_bf, mask_kq = ph.sb("ident_bf", [P, P], BF16), ph.sb("mask_kq", [P, P], BF16)
        mask = ph.sb("mask", [P, CH])
        junk = ph.sb("junk", [P, RING, CH], BF16)
        PR = ph.sb("PR", [P, 4, 4, CH])
        mxp = ph.sb("mxp", [P, R, 4, ST, 2])
        nmax = ph.sb("nmax", [P, 4 * ST])
        mhi = ph.sb("mhi", [4 * ST, R, P], F32R)
        mlo = ph.sb("mlo", [4 * ST, R, P], F32R)
        OT = ph.sb("OT", [P, 2, CH])
        rec = ph.sb("rec", [P, 2, TPC, 4])
        s1 = ph.psum("s1", [P, RING, CH])
        s2 = ph.psum("s2", [P, RING, CH])
        o = ph.psum("o", [P, 2, CH])
        rows_set = ph.sem("rows_set")
        cleared, m_in, vs_in, mxp_set = (ph.sem(n) for n in ("cleared", "m_in", "vs_in", "mxp_set"))
        went = ph.sem("went")
        qk_in = [ph.sem(f"qk_in{u}") for u in range(R)]
        s1_full, s1_free, m_red, mhi_ok = (ph.sem(n) for n in ("s1_full", "s1_free", "m_red", "mhi_ok"))
        s2_full, p_ready, pv_done = (ph.sem(n) for n in ("s2_full", "p_ready", "pv_done"))
        ot_ready, ox_full, recd, o_free = (ph.sem(n) for n in ("ot_ready", "ox_full", "recd", "o_free"))
        loads_per_quad = 16 * 7

        def number(q):
            j, r = q
            return R * j + r

        def ring(q):
            return q[1] % R

        def nxt(q, by=1):
            return q[0], q[1] + by

        def step1(q, n):
            r = q[1]
            if known(q, 1):
                at = len(chunks) if n is None else n
            elif n is None:
                at = n1 * r + early + late + (0 if is_end(q, 1) else TURN_AFTER)
            elif n >= early:
                at = n1 * r + n
            elif known(q, 2):
                at = n1 + n
            else:
                at = n1 * (r - 1) + early + late + n + (n >= TURN_AFTER)
            return at

        def count1(q, n, more=1):
            return n1 * R * q[0] + (step1(q, n) + more)

        def bank1(q, n):
            return step1(q, n) % RING

        def bank2(q, n, h):
            return (4 * nu * q[1] + 4 * n + h) % RING

        def known(q, below):
            return isinstance(q[0], int) and number(q) < below

        def over_quads(eng, quad):
            quad((0, 0))
            with eng.Fori(0, (NQ - 3) // R) as j:
                for r in range(R):
                    quad((j, 1 + r))
            for n in range(1 + (NQ - 3) // R * R, NQ):
                quad((0, n))

        def is_last(q):
            return isinstance(q[0], int) and number(q) == NQ - 1

        with nc.Block() as block:
            @block.sync
            def _(sp):
                def load(q):
                    u, i = ring(q), number(q)
                    for part, row in ((0, 0), (1, dh), (0, 2 * dh)):
                        sp.dma_start(f(Q[u][row:row + dh, :, :]),
                                     q_scr[part, bass.ds(i, 1)].rearrange("o h p n -> p (o h) n")).then_inc(qk_in[u], 16)
                    sp.dma_start(f(Q[u][mrow:mrow + 2, :, :]), f(Q[u][ROWS - 2:ROWS, :, :])).then_inc(qk_in[u], 16)
                    for part, row in ((0, 0), (0, dh), (1, 2 * dh)):
                        sp.dma_start(f(K[u][row:row + dh, :, :]),
                                     k_scr[part, bass.ds(i, 1)].rearrange("o h p n -> p (o h) n")).then_inc(qk_in[u], 16)

                def maxima(q):
                    u = ring(q)
                    sp.wait_ge(s1_free, count1(q, None))
                    sp.dma_start(f(Q[u][mrow:mrow + 1, :, :]), f(mhi[:, u, :])).then_inc(m_in, 16)
                    sp.dma_start(f(Q[u][mrow + 1:mrow + 2, :, :]), f(mlo[:, u, :])).then_inc(m_in, 16)

                def quad(q):
                    if not (isinstance(q[0], int) and number(q) + 2 >= NQ):
                        if not known(q, 1):
                            sp.wait_ge(s2_full, 4 * nu * number(q))
                        else:
                            sp.wait_ge(rows_set, 2 * R - 2)
                        load(nxt(q, 2))
                    if not is_last(q):
                        maxima(nxt(q))

                load((0, 0))
                sp.wait_ge(rows_set, 2)
                load((0, 1))
                maxima((0, 0))
                over_quads(sp, quad)

            @block.gpsimd
            def _(pool):
                for v in range(R):
                    pool.memset(VS[v][:, :, :, :], 0.0).then_inc(cleared, 1)
                pool.tensor_copy(ident_bf[:, :], ident[:, :]).then_inc(cleared, 1)
                pool.tensor_copy(mask_kq[:, :], masks[1][:, :]).then_inc(cleared, 1)
                pool.wait_ge(cleared, R + 2)
                for v in range(R):
                    pool.memset(VS[v][:, :, :, dh:dh + 1], 1.0).then_inc(cleared, 1)
                for u in range(1, R):
                    set_constant_rows(pool, (Q[u], K[u]), rows_set)
                pool.wait_ge(cleared, 2 * R + 2)

                def values(q):
                    src = V[:, bass.ds(number(q), 1), :, :].rearrange("p o k (h c) -> p (o k) h c", h=kh)
                    pool.tensor_copy(VS[ring(q)][:, :, :, 0:dh], src).then_inc(vs_in, 1)

                for n in range(R):
                    values((0, n))
                def quad(q):
                    i = number(q)
                    for n in range(nu):
                        if n == LAG + 1 and not known(q, 1) and not (isinstance(q[0], int) and number(q) + 2 >= NQ):
                            pool.wait_ge(pv_done, 4 + nu * i)
                            values(nxt(q, 2))

                over_quads(pool, quad)

            @block.tensor
            def _(pe):
                def scores1(q, n):
                    u = ring(q)
                    h, qt, kc = chunks[n]
                    if not (known(q, 1) and n < RING):
                        pe.wait_ge(s1_free, count1(q, n, 1 - RING))
                    cols = width(n)
                    wide = max(cols, 2 * P)
                    pe.matmul(s1[:, bank1(q, n), 0:wide], Q[u][0:ROWS, h, qt * P:(qt + 1) * P],
                              K[u][0:ROWS, h % kh, kc * CH:kc * CH + wide], start=True, stop=True).then_inc(s1_full, 1)

                def turn_maxima(q):
                    pe.wait_ge(m_red, nth(number(q)))
                    pe.wait_ge(s1_free, count1(q, None, 1 - RING))
                    pe.transpose(s1[0:4 * ST, bank1(q, None), 0:P], nmax[:, :], ident[:, :]).then_inc(s1_full, 1)

                def scores2(q, n, h):
                    u, bank = ring(q), bank2(q, n, h)
                    c, kt = units[n]
                    q0, first = span(c, kt)
                    pe.wait_ge(p_ready, 4 * nu * number(q) + (4 * n + h + 1))
                    ins = pe.matmul(s2[:, bank, first:CH], K[u][0:ROWS, h % kh, kt * P:(kt + 1) * P],
                                    Q[u][0:ROWS, h, c * CH + first:(c + 1) * CH], start=True, stop=not diagonal(n))
                    if diagonal(n):
                        ins = pe.matmul(s2[:, bank, q0:q0 + P], ident_bf[:, :], mask_kq[:, :], start=False, stop=True)
                    ins.then_inc(s2_full, 1)

                def product(q, n):
                    u, i = ring(q), number(q)
                    c, kt = units[n]
                    q0, _ = span(c, kt)
                    pe.wait_ge(p_ready, 4 * nu * i + (4 * n + 4 + RING))
                    if kt == 0:
                        pe.wait_ge(o_free, two_back(2 * i + c))
                    if n == 0:
                        pe.wait_ge(vs_in, nth(i))
                    for h in range(4):
                        ins = pe.matmul(o[32 * h:32 * h + 32, c, q0:CH], VS[u][:, kt, h % kh, :],
                                        PR[:, n % 4, h, q0:CH], start=kt == 0, stop=n in ends)
                    ins.then_inc(pv_done, 1)

                def turn_outputs(q, c):
                    pe.wait_ge(ot_ready, nth(2 * number(q) + c))
                    for t in range(TPC):
                        ins = pe.transpose(o[:, c, t * P:(t + 1) * P], OT[:, c, t * P:(t + 1) * P], ident[:, :])
                    ins.then_inc(ox_full, 1)

                def quad(q):
                    pe.wait_ge(m_in, 32 * (number(q) + 1))
                    after, second = nxt(q), nxt(q, 2)

                    def begin(m):
                        if m == 0:
                            pe.wait_ge(qk_in[ring(second)], loads_per_quad * (second[0] + (second[1] // R + 1)))
                        scores1(second, m)

                    def gap(g):
                        in_gap(g, q, lambda m: scores1(after, m), begin, lambda: turn_maxima(after))

                    for n in range(nu):
                        for h in range(4):
                            scores2(q, n, h)
                            gap(G * n + h + (h > AT))
                            if h == AT:
                                if n >= LAG:
                                    product(q, n - LAG)
                                elif not known(q, 1):
                                    product(nxt(q, -1), nu + n - LAG)
                                gap(G * n + AT + 1)
                        if n == LAG and not known(q, 1):
                            turn_outputs(nxt(q, -1), 1)
                        if n == ends[0] + LAG + 1:
                            turn_outputs(q, 0)
                    if is_last(q):
                        for n in range(nu - LAG, nu):
                            product(q, n)
                        turn_outputs(q, 1)

                pe.sem_inc(pv_done, 4)
                pe.wait_ge(qk_in[0], loads_per_quad)
                for n in range(len(chunks)):
                    scores1((0, 0), n)
                turn_maxima((0, 0))
                pe.wait_ge(qk_in[1], loads_per_quad)
                for n in range(early):
                    scores1((0, 1), n)
                pe.wait_ge(cleared, 2 * R + 2)
                over_quads(pe, quad)

            @block.scalar
            def _(act):
                act.sem_inc(p_ready, RING)

                def outputs(q, c):
                    act.wait_ge(pv_done, 4 + nu * number(q) + (ends[c] + 1))
                    act.activation(OT[:, c, :], o[:, c, :], ACT.Copy).then_inc(ot_ready, 1)

                def quad(q):
                    for n, (c, kt) in enumerate(units):
                        q0, _ = span(c, kt)
                        act.wait_ge(pv_done, nu * number(q) + (n + 1))
                        for h in range(4):
                            act.wait_ge(s2_full, 4 * nu * number(q) + (4 * n + h + 1))
                            act.activation(PR[:, n % 4, h, q0:CH], s2[:, bank2(q, n, h), q0:CH], ACT.Exp,
                                           scale=scale).then_inc(p_ready, 1)
                        if n == LAG - 1 and not known(q, 1):
                            outputs(nxt(q, -1), 1)
                        if n == ends[0] + LAG:
                            outputs(q, 0)
                    if is_last(q):
                        outputs(q, 1)

                over_quads(act, quad)

            @block.vector
            def _(dve):
                def maximum(q, n):
                    h, qt, kc = chunks[n]
                    cols = width(n)
                    dve.wait_ge(s1_full, count1(q, n))
                    bank, to = bank1(q, n), mxp[:, ring(q), h, qt, kc:kc + 1]
                    if causal and (qt + 1) * P <= (kc + 1) * CH:
                        dve.sem_inc(went, 1)
                        dve.tensor_tensor_reduce(junk[:, bank, 0:cols], s1[:, bank, 0:cols], mask[:, CH - cols:CH], 1.0, NEG,
                                                 ALU.add, ALU.max, to).then_inc(s1_free, 1)
                    else:
                        dve.tensor_reduce(to, s1[:, bank, 0:cols], AX.X, ALU.max).then_inc(s1_free, 1)

                def negated(q):
                    dve.wait_ge(s1_free, count1(q, len(chunks) - 1))
                    dve.tensor_reduce(nmax[:, :], mxp[:, ring(q), :, :, :].rearrange("p h q k -> p (h q) k"), AX.X,
                                      ALU.max, negate=True).then_inc(m_red, 1)

                def maxima(q):
                    i, u = number(q), ring(q)
                    turned = s1[0:4 * ST, bank1(q, None), 0:P]
                    dve.wait_ge(s1_full, count1(q, None))
                    if not known(q, 1):
                        dve.wait_ge(m_in, 32 * i)
                    dve.tensor_copy(mhi[:, u, :], turned[:, :]).then_inc(mhi_ok, 1)
                    dve.wait_ge(mhi_ok, nth(i))
                    dve.tensor_tensor(mlo[:, u, :], turned[:, :], f(mhi[:, u, :]),
                                      ALU.subtract).then_inc(s1_free, 1)

                def normalised(q, c):
                    i = number(q)
                    dve.wait_ge(ox_full, nth(2 * i + c))
                    turned = o[:, c, :].rearrange("p (t h e) -> p t h e", t=TPC, h=4)
                    dve.reciprocal(rec[:, c, :, :], turned[:, :, :, dh]).then_inc(recd, 1)
                    dve.wait_ge(recd, nth(2 * i + c))
                    for t in range(TPC):
                        dst = O[:, c * TPC + t, bass.ds(i, 1), :].rearrange("p o (h e) -> p (o h) e", h=4)
                        ins = dve.tensor_tensor(dst, turned[:, t, :, 0:dh],
                                                rec[:, c, t, :].unsqueeze(2).broadcast_to([P, 4, dh]), ALU.mult)
                    ins.then_inc(o_free, 1)

                def quad(q):
                    after, second = nxt(q), nxt(q, 2)

                    def chunk(m):
                        maximum(after, m)
                        if m == len(chunks) - 1:
                            negated(after)

                    for g in range(gaps):
                        in_gap(g, q, chunk, lambda m: maximum(second, m), lambda: maxima(after))
                        if g == G * LAG + 4 and not known(q, 1):
                            normalised(nxt(q, -1), 1)
                        if g == G * (ends[0] + LAG + 1) + 4:
                            normalised(q, 0)
                    if is_last(q):
                        normalised(q, 1)

                dve.sem_inc(o_free, CREDIT)
                dve.memset(mxp[:, :, :, :, :], NEG).then_inc(mxp_set, 1)
                dve.memset(mask[:, 0:CH - P], 0.0).then_inc(mxp_set, 1)
                dve.tensor_copy(mask[:, CH - P:CH], mask_qk[:, :]).then_inc(mxp_set, 1)
                dve.wait_ge(mxp_set, 3)
                for n in range(len(chunks)):
                    maximum((0, 0), n)
                negated((0, 0))
                maxima((0, 0))
                for n in range(early):
                    maximum((0, 1), n)
                over_quads(dve, quad)


def out_projection(nc, name, X, O, ident, weight, bias=None):
    quads = O.shape[2] // B
    whi, wlo = weight.hi, weight.lo
    with Phase(nc, name) as ph:
        bb = ph.sb("bb", [P, D])
        ohi, olo = ph.sb("ohi", [P, 2, KT, P], F32R), ph.sb("olo", [P, 2, KT, P], F32R)
        turned = ph.psum("turned", [P, 2, CH])
        py = ph.psum("py", [P, 2, CH])
        loaded, added = ph.sem("loaded"), ph.sem("added")
        turn, hi_ok, lo_ok, mul, out = (ph.sem(n) for n in ("turn", "hi_ok", "lo_ok", "mul", "out"))
        with nc.Block() as block:
            @block.sync
            def _(sp):
                if bias is not None:
                    sp.dma_start(bb[:, :], bias.partition_broadcast(P)).then_inc(loaded, 16)

            @block.gpsimd
            def _(pool):
                if bias is not None:
                    pool.wait_ge(loaded, 16)
                    for t in range(NT):
                        pool.tensor_tensor(X[:, t, :], X[:, t, :], bb[:, :], ALU.add).then_inc(added, 1)

            @block.tensor
            def _(pe):
                def turned_tile(n):
                    b, t = n // ST, n % ST
                    if n >= 2:
                        pe.wait_ge(lo_ok, n - 1)
                    for k in range(KT):
                        src = O[:, t, b * quads + k * quads // KT:b * quads + (k + 1) * quads // KT, :]
                        ins = pe.transpose(turned[:, n % 2, k * P:(k + 1) * P], src.rearrange("p g c -> p (g c)"), ident[:, :])
                    ins.then_inc(turn, 1)

                turned_tile(0)
                for n in range(NT):
                    if n + 1 < NT:
                        turned_tile(n + 1)
                    pe.wait_ge(lo_ok, n + 1)
                    if n >= 2:
                        pe.wait_ge(out, n - 1)
                    three_terms(pe, py[:, n % 2, 0:D],
                                [((ohi[:, n % 2, k, :], olo[:, n % 2, k, :]), (whi[:, k, :], wlo[:, k, :]))
                                 for k in range(KT)]).then_inc(mul, 1)

            @block.scalar
            def _(act):
                for n in range(NT):
                    act.wait_ge(turn, n + 1)
                    if n >= 2:
                        act.wait_ge(mul, n - 1)
                    act.activation(ohi[:, n % 2, :, :].rearrange("p k n -> p (k n)"), turned[:, n % 2, 0:D],
                                   ACT.Copy).then_inc(hi_ok, 1)

            @block.vector
            def _(dve):
                def summed(n):
                    dve.wait_ge(mul, n + 1)
                    if bias is not None:
                        dve.wait_ge(added, n + 1)
                    dve.tensor_tensor(X[:, n, :], py[:, n % 2, 0:D], X[:, n, :], ALU.add).then_inc(out, 1)

                for n in range(NT):
                    dve.wait_ge(hi_ok, n + 1)
                    dve.tensor_tensor(olo[:, n % 2, :, :].rearrange("p k n -> p (k n)"), turned[:, n % 2, 0:D],
                                      f(ohi[:, n % 2, :, :]).rearrange("p k n -> p (k n)"),
                                      ALU.subtract).then_inc(lo_ok, 1)
                    if n >= 1:
                        summed(n - 1)
                summed(NT - 1)


def gated_ffn(nc, name, X, xn, ident, experts, rest):
    xhi, xlo = xn
    E, W1, ahead = experts.w1.shape[0], experts.w1.shape[2], experts.ahead
    w1hi, w1lo, w2hi, w2lo = experts.w1hi, experts.w1lo, experts.w2hi, experts.w2lo
    gate_w, ghi, glo = experts.gate, None, None
    if gate_w is not None:
        ghi, glo = experts.ghi, experts.glo
    K2 = 2 if rest else 1
    tiles = 3 if rest else 2
    UO = 64
    EX = E - 1
    RH = 3 if 2 * E % 3 == 0 else 4
    with Phase(nc, name) as ph:
        experts.semaphores(ph)
        sg = ph.sb("sg", [P, 2, 2, CH])
        hf = ph.sb("hf", [P, 2, K2, CH])
        hhi, hlo = ph.sb("hhi", [P, RH, K2, CH], F32R), ph.sb("hlo", [P, RH, K2, CH], F32R)
        pg = [ph.psum(f"pg{u}", [P, 3, CH]) for u in range(2)]
        py = ph.psum("py", [P, TPC, D])
        zeroed = ph.sem("zeroed")
        zeros = 3 if gate_w is not None else 2
        g_full, sg_ok, h_ok, hi_ok, lo_ok, y_full, y_out = (
            ph.sem(n) for n in ("g_full", "sg_ok", "h_ok", "hi_ok", "lo_ok", "y_full", "y_out"))
        if gate_w is not None:
            lt = ph.sb("lt", [EX, NCH, CH])
            lg = ph.sb("lg", [P, NT, EX])
            small = ph.sb("small", [P, 2, NT])
            top = ph.sb("top", [P, NT, 8])
            topi = ph.sb("topi", [P, NT, 8], mybir.dt.uint32)
            topf = ph.sb("topf", [P, NT, 2])
            number = ph.sb("number", [P, NT, EX])
            chosen = ph.sb("chosen", [P, 2, NT, EX])
            cw = ph.sb("cw", [P, NT, E])
            gcut, gmul, glt, gturn, gs, gexp = (
                ph.sem(n) for n in ("gcut", "gmul", "glt", "gturn", "gs", "gexp"))
        with nc.Block() as block:
            @block.sync
            def _(sp):
                experts.load(sp, ahead, E)

            @block.gpsimd
            def _(pool):
                if gate_w is not None:
                    pool.memset(cw[:, :, :], 1.0).then_inc(zeroed, 1)
                if rest:
                    pool.memset(hhi[:, :, 1, :].bitcast(F32), 0.0).then_inc(zeroed, 1)
                    pool.memset(hlo[:, :, 1, :].bitcast(F32), 0.0).then_inc(zeroed, 1)
                experts.cut(pool, ahead, E)

            @block.tensor
            def _(pe):
                if gate_w is not None:
                    for c in range(NCH):
                        at = slice(c * CH, (c + 1) * CH)
                        three_terms(pe, pg[c % 2][:, c // 2, :],
                                    [((ghi[:, k, :], glo[:, k, :]), (xhi[:, k, at], xlo[:, k, at]))
                                     for k in range(KT)]).then_inc(gmul, 1)
                    pe.wait_ge(glt, NCH)
                    for t in range(NT):
                        ins = pe.transpose(pg[0][:, 2, t * EX:(t + 1) * EX], lt[:, t // TPC, (t % TPC) * P:(t % TPC + 1) * P],
                                           ident[0:EX, 0:EX])
                    ins.then_inc(gturn, 1)
                    pe.wait_ge(gs, 1)

                def hidden(j, k):
                    n, e = 2 * E * j + k, k % E
                    at = bass.ds(2 * CH * j + CH * (k // E), CH)
                    if ahead <= k < E:
                        pe.wait_ge(experts.lo_cut, k - ahead + 1)
                    pe.wait_ge(h_ok, two_back(n))
                    for m in range(tiles):
                        cs = slice(m * P, (m + 1) * P) if m < 2 else slice(2 * P, W1)
                        ins = three_terms(pe, pg[k % 2][0:cs.stop - cs.start, m, :],
                                          [((w1hi[:, e, q, cs], w1lo[:, e, q, cs]), (xhi[:, q, at], xlo[:, q, at]))
                                           for q in range(KT)])
                    ins.then_inc(g_full, 1)

                def down(j, k):
                    n, e = 2 * E * j + k, k % E
                    pe.wait_ge(lo_ok, nth(n))
                    pe.wait_ge(y_out, nth(n))
                    if rest:
                        pe.wait_ge(zeroed, zeros)
                    for t in range(TPC):
                        ts = slice(t * P, (t + 1) * P)
                        ins = three_terms(pe, py[:, t, :],
                                          [((hhi[0:(P, ROWS)[q], k % RH, q, ts], hlo[0:(P, ROWS)[q], k % RH, q, ts]),
                                            (w2hi[0:(P, ROWS)[q], e, q, :], w2lo[0:(P, ROWS)[q], e, q, :]))
                                           for q in range(K2)])
                    ins.then_inc(y_full, 1)

                pe.sem_inc(y_full, RH)
                with pe.Fori(0, NCH // 2) as j:
                    for k in range(2 * E):
                        hidden(j, k)
                        if k >= 2:
                            down(j, k - 2)
                    down(j, 2 * E - 2)
                    down(j, 2 * E - 1)

            @block.scalar
            def _(act):
                if gate_w is not None:
                    act.wait_ge(gs, 2)
                    act.activation(lg[:, :, :], lg[:, :, :], ACT.Exp).then_inc(gexp, 1)
                if rest:
                    act.wait_ge(zeroed, zeros)
                with act.Fori(0, NCH // 2) as j:
                    for k in range(2 * E):
                        n, h = 2 * E * j + k, k % 2
                        act.wait_ge(g_full, nth(n))
                        act.wait_ge(h_ok, two_back(n))
                        ins = act.activation(sg[:, h, 0, :], pg[h][:, 0, :], ACT.Silu)
                        if rest:
                            ins = act.activation(sg[UO:UO + 48, h, 1, :], pg[h][0:48, 2, :], ACT.Silu)
                        ins.then_inc(sg_ok, 1)
                        act.wait_ge(h_ok, cnth(n))
                        act.wait_ge(y_full, n + 1)
                        ins = act.activation(hhi[:, k % RH, 0, :], hf[:, h, 0, :], ACT.Copy)
                        if rest:
                            ins = act.activation(hhi[0:48, k % RH, 1, :], hf[0:48, h, 1, :], ACT.Copy)
                        ins.then_inc(hi_ok, 1)

            @block.vector
            def _(dve):
                dve.sem_inc(h_ok, CREDIT)
                dve.sem_inc(y_out, 1)
                if gate_w is not None:
                    dve.wait_ge(zeroed, 1)
                    for c in range(NCH):
                        dve.wait_ge(gmul, c + 1)
                        dve.tensor_copy(lt[:, c, :], pg[c % 2][0:EX, c // 2, :]).then_inc(glt, 1)
                    dve.wait_ge(gturn, 1)
                    dve.tensor_copy(lg[:, :, :], pg[0][:, 2, 0:NT * EX].rearrange("p (t e) -> p t e", e=EX)).then_inc(gs, 1)
                    dve.wait_ge(gs, 1)
                    dve.tensor_reduce(small[:, 0, :], lg[:, :, :], AX.X, ALU.max).then_inc(gcut, 1)
                    dve.wait_ge(gcut, 1)
                    wide = lambda v: v.unsqueeze(2).broadcast_to([P, NT, EX])
                    dve.tensor_tensor(lg[:, :, :], lg[:, :, :], wide(small[:, 0, :]), ALU.subtract).then_inc(gs, 1)
                    dve.wait_ge(gexp, 1)
                    dve.tensor_reduce(small[:, 0, :], lg[:, :, :], AX.X, ALU.add).then_inc(gcut, 1)
                    dve.wait_ge(gcut, 2)
                    dve.reciprocal(small[:, 1, :], small[:, 0, :]).then_inc(gcut, 1)
                    dve.wait_ge(gcut, 3)
                    dve.tensor_tensor(lg[:, :, :], lg[:, :, :], wide(small[:, 1, :]), ALU.mult).then_inc(gcut, 1)
                    dve.wait_ge(gcut, 4)
                    for t in range(NT):
                        ins = dve.max(top[:, t, :], lg[:, t, :])
                    ins.then_inc(gcut, 1)
                    dve.wait_ge(gcut, 5)
                    dve.tensor_tensor(small[:, 0, :], top[:, :, 0], top[:, :, 1], ALU.add).then_inc(gcut, 1)
                    for t in range(NT):
                        ins = dve.max_index(topi[:, t, :], top[:, t, :], lg[:, t, :])
                    ins.then_inc(gcut, 1)
                    for e in range(EX):
                        ins = dve.memset(number[:, :, e:e + 1], float(e))
                    ins.then_inc(gcut, 1)
                    dve.wait_ge(gcut, 8)
                    dve.tensor_scalar(small[:, 0, :], small[:, 0, :], 1e-20, None, ALU.add).then_inc(gcut, 1)
                    dve.tensor_copy(topf[:, :, :], topi[:, :, 0:2]).then_inc(gcut, 1)
                    dve.wait_ge(gcut, 10)
                    dve.reciprocal(small[:, 1, :], small[:, 0, :]).then_inc(gcut, 1)
                    for m in range(2):
                        dve.tensor_tensor(chosen[:, m, :, :], number[:, :, :], wide(topf[:, :, m]),
                                          ALU.is_equal).then_inc(gcut, 1)
                    dve.wait_ge(gcut, 13)
                    dve.tensor_tensor(chosen[:, 0, :, :], chosen[:, 0, :, :], chosen[:, 1, :, :], ALU.add).then_inc(gcut, 1)
                    dve.wait_ge(gcut, 14)
                    dve.tensor_tensor(lg[:, :, :], lg[:, :, :], chosen[:, 0, :, :], ALU.mult).then_inc(gcut, 1)
                    dve.wait_ge(gcut, 15)
                    dve.tensor_tensor(cw[:, :, 0:EX], lg[:, :, :], wide(small[:, 1, :]), ALU.mult).then_inc(gcut, 1)
                    dve.wait_ge(gcut, 16)
                if rest:
                    dve.wait_ge(zeroed, zeros)

                def add(j, k):
                    n, e = 2 * E * j + k, k % E
                    dve.wait_ge(y_full, n + (1 + RH))
                    if gate_w is None:
                        tok = bass.ds(2 * TPC * j + TPC * (k // E), TPC)
                        ins = dve.tensor_tensor(X[:, tok, :], py[:, :, :], X[:, tok, :], ALU.add)
                    else:
                        for t in range(TPC):
                            tok = bass.ds(2 * TPC * j + (TPC * (k // E) + t), 1)
                            x = X[:, tok, :].rearrange("p o d -> p (o d)")
                            ins = dve.scalar_tensor_tensor(out=x, in0=py[:, t, :], scalar=cw[:, tok, e],
                                                           in1=x, op0=ALU.mult, op1=ALU.add)
                    ins.then_inc(y_out, 1)

                with dve.Fori(0, NCH // 2) as j:
                    for k in range(2 * E):
                        n, h = 2 * E * j + k, k % 2
                        dve.wait_ge(sg_ok, nth(n))
                        ins = dve.tensor_tensor(hf[:, h, 0, :], sg[:, h, 0, :], pg[h][:, 1, :], ALU.mult)
                        if rest:
                            ins = dve.tensor_tensor(hf[0:48, h, 1, :], sg[UO:UO + 48, h, 1, :], pg[h][UO:UO + 48, 2, :],
                                                    ALU.mult)
                        ins.then_inc(h_ok, 1)
                        if k >= 2:
                            add(j, k - 2)
                        dve.wait_ge(hi_ok, nth(n))
                        r = k % RH
                        ins = dve.tensor_tensor(hlo[:, r, 0, :], hf[:, h, 0, :], f(hhi[:, r, 0, :]), ALU.subtract)
                        if rest:
                            ins = dve.tensor_tensor(hlo[0:48, r, 1, :], hf[0:48, h, 1, :], f(hhi[0:48, r, 1, :]),
                                                    ALU.subtract)
                        ins.then_inc(lo_ok, 1)
                    add(j, 2 * E - 2)
                    add(j, 2 * E - 1)


def hadamard_down(nc, name, ident, w2t, scr, x, X):
    NB = w2t.shape[0] // P
    with Phase(nc, name) as ph:
        w = [ph.sb(f"w{u}", [P, NB, D]) for u in range(2)]
        h = [ph.sb(f"h{u}", [P, P]) for u in range(2)]
        out = ph.sb("out", [P, NB, D])
        acc = ph.psum("acc", [P, NB, D])
        x_in = ph.sem("x_in")
        loaded, step, mul, scaled, stored = (ph.sem(n) for n in ("loaded", "step", "mul", "scaled", "stored"))
        with nc.Block() as block:
            @block.sync
            def _(sp):
                sp.dma_start(w[0][:, :, :], w2t.rearrange("(k p) n -> p k n", p=P)).then_inc(loaded, 16)
                sp.dma_start(X[:, :, :], x.rearrange("b (n p) d -> p (b n) d", p=P)).then_inc(x_in, 16)
                sp.wait_ge(scaled, 1)
                sp.dma_start(scr.rearrange("k o p n -> p (k o) n"), out[:, :, :]).then_inc(stored, 16)
                sp.wait_ge(stored, 16)
                sp.wait_ge(x_in, 16)

            @block.vector
            def _(dve):
                done, at = 0, 0
                dve.tensor_copy(h[0][:, :], ident[:, :]).then_inc(step, 1)
                done += 1
                g = 1
                while g < P:
                    dve.wait_ge(step, done)
                    a = h[at][:, :].rearrange("p (m two g) -> p m two g", two=2, g=g)
                    c = h[1 - at][:, :].rearrange("p (m two g) -> p m two g", two=2, g=g)
                    dve.tensor_tensor(c[:, :, 0, :], a[:, :, 0, :], a[:, :, 1, :], ALU.add).then_inc(step, 1)
                    dve.tensor_tensor(c[:, :, 1, :], a[:, :, 0, :], a[:, :, 1, :], ALU.subtract).then_inc(step, 1)
                    done, at, g = done + 2, 1 - at, 2 * g
                dve.wait_ge(loaded, 16)
                g, bt = 1, 0
                while g < NB:
                    dve.wait_ge(step, done)
                    a = w[bt][:, :, :].rearrange("p (m two g) n -> p m two (g n)", two=2, g=g)
                    c = w[1 - bt][:, :, :].rearrange("p (m two g) n -> p m two (g n)", two=2, g=g)
                    dve.tensor_tensor(c[:, :, 0, :], a[:, :, 0, :], a[:, :, 1, :], ALU.add).then_inc(step, 1)
                    dve.tensor_tensor(c[:, :, 1, :], a[:, :, 0, :], a[:, :, 1, :], ALU.subtract).then_inc(step, 1)
                    done, bt, g = done + 2, 1 - bt, 2 * g

            @block.tensor
            def _(pe):
                pe.wait_ge(step, 1 + 2 * 7 + 2 * 3)
                for q in range(NB // 2):
                    ins = pe.matmul(acc[:, 2 * q:2 * q + 2, :], h[1][:, :], w[1][:, 2 * q:2 * q + 2, :],
                                    start=True, stop=True)
                ins.then_inc(mul, 1)

            @block.scalar
            def _(act):
                act.wait_ge(mul, 1)
                act.activation(out[:, :, :], acc[:, :, :], ACT.Copy, scale=float(NB * P) ** -0.5).then_inc(scaled, 1)


def wide_attention(nc, name, X, xn, ident, weight, b_qk, b_v, out_weight, b_out):
    whi, wlo, ohi, olo = weight.hi, weight.lo, out_weight.hi, out_weight.lo
    xhi, xlo = xn
    scale = float(D) ** -0.5
    NHALF = S // CH
    with Phase(nc, name) as ph:
        bias = ph.sb("bias", [P, 4])
        vb, ob = ph.sb("vb", [P, D]), ph.sb("ob", [P, D])
        qkhi, qklo = ph.sb("qkhi", [P, 2, KT, S], F32R), ph.sb("qklo", [P, 2, KT, S], F32R)
        vhi, vlo = ph.sb("vhi", [P, ST, D], F32R), ph.sb("vlo", [P, ST, D], F32R)
        vx = ph.sb("vx", [P, ST, 2, KT, P], F32R)
        vf = ph.sb("vf", [P, 2, D])
        pr = ph.sb("pr", [P, 2, S])
        neg = ph.sb("neg", [P, 2, 2])
        sums, inv = ph.sb("sums", [P, 2, TPC]), ph.sb("inv", [P, 2, TPC])
        pthi, ptlo = ph.sb("pthi", [P, ST, CH], F32R), ph.sb("ptlo", [P, ST, CH], F32R)
        chi, clo = ph.sb("chi", [P, KT, CH], F32R), ph.sb("clo", [P, KT, CH], F32R)
        work = ph.psum("work", [P, 2, CH])
        sc = ph.psum("sc", [P, 2, S])
        turned = ph.psum("turned", [P, ST, P])
        loaded, based = ph.sem("loaded"), ph.sem("based")
        work_full, work_free, vcopy, own = (ph.sem(n) for n in ("work_full", "work_free", "vcopy", "own"))
        cut_hi, vf_ok, v_ok = (ph.sem(n) for n in ("cut_hi", "vf_ok", "v_ok"))
        sc_full, max_ok, exp_ok, turn_full, pt_hi, pt_lo = (
            ph.sem(n) for n in ("sc_full", "max_ok", "exp_ok", "turn_full", "pt_hi", "pt_lo"))
        loads = [(bias[:, :], b_qk[:, 0:2 * KT]),
                 (vb[:, :], b_v.partition_broadcast(P)),
                 (ob[:, :], b_out.partition_broadcast(P))]
        QK = [(w, m, c) for w in range(2) for m in range(KT) for c in range(NHALF)]
        AT_V = len(QK)
        AT_C = [AT_V + ST + half * (KT + TPC) for half in range(NHALF)]
        STEPS = AT_V + ST + NHALF * (KT + TPC)
        AT_CH = [AT_V + ST + half * KT for half in range(NHALF)]
        HIS = AT_V + ST + NHALF * KT
        OWN = ST + NHALF

        def in_order(scores, turn, context, output, turn_first=False):
            scores(0)
            for t in range(1, ST):
                if turn_first and t != TPC + 1:
                    turn(t - 1)
                    scores(t)
                else:
                    scores(t)
                    if t == TPC + 1:
                        context(0)
                    turn(t - 1)
                if t == TPC + 2:
                    output(0)
            turn(ST - 1)
            context(1)
            output(1)

        with nc.Block() as block:
            @block.sync
            def _(sp):
                for dst, src in loads:
                    sp.dma_start(dst, src).then_inc(loaded, 16)

            @block.gpsimd
            def _(pool):
                with pool.Fori(0, B) as b:
                    for t in range(ST):
                        pool.wait_ge(work_full, STEPS * b + (AT_V + t + 1))
                        at = bass.ds(S * b + t * P, P)
                        pool.tensor_copy(vx[:, t, 0, :, :], f(xhi[:, :, at]))
                        pool.tensor_copy(vx[:, t, 1, :, :], f(xlo[:, :, at])).then_inc(vcopy, 1)

            @block.tensor
            def _(pe):
                pe.sem_inc(work_full, STEPS)
                with pe.Fori(0, B) as b:
                    def step(at, out, pairs):
                        pe.wait_ge(work_free, two_back(STEPS * b + at))
                        three_terms(pe, out, pairs).then_inc(work_full, 1)

                    for n, (w, m, c) in enumerate(QK):
                        cs = slice(w * D + m * P, w * D + (m + 1) * P)
                        at = bass.ds(S * b + c * CH, CH)
                        step(n, work[:, n % 2, :], [((whi[:, k, cs], wlo[:, k, cs]), (xhi[:, k, at], xlo[:, k, at]))
                                                    for k in range(KT)])
                    for t in range(ST):
                        n = AT_V + t
                        pe.wait_ge(vcopy, ST * b + (t + 1))
                        pe.wait_ge(work_free, two_back(STEPS * b + n))
                        pairs = [((vx[:, t, 0, k, :], vx[:, t, 1, k, :]),
                                  (whi[:, k, 2 * D:3 * D], wlo[:, k, 2 * D:3 * D])) for k in range(KT)]
                        three_terms(pe, work[:, n % 2, 0:D], pairs).then_inc(work_full, 1)
                    pe.wait_ge(work_free, cnth(STEPS * b + (AT_V - 1)))

                    def scores(t):
                        g = ST * b + t
                        pe.wait_ge(exp_ok, two_back(g))
                        ts = slice(t * P, (t + 1) * P)
                        for c in range(NHALF):
                            cs = slice(c * CH, (c + 1) * CH)
                            ins = three_terms(pe, sc[:, t % 2, cs],
                                              [((qkhi[:, 0, k, ts], qklo[:, 0, k, ts]),
                                                (qkhi[:, 1, k, cs], qklo[:, 1, k, cs])) for k in range(KT)])
                        ins.then_inc(sc_full, 1)

                    def turn(t):
                        g = ST * b + t
                        pe.wait_ge(exp_ok, cnth(g))
                        pe.wait_ge(pt_lo, g + 1)
                        for k in range(ST):
                            ins = pe.transpose(turned[:, k, :], pr[:, t % 2, k * P:(k + 1) * P], ident[:, :])
                        ins.then_inc(turn_full, 1)

                    def context(half):
                        pe.wait_ge(pt_lo, ST * b + (TPC * (half + 1) + 1))
                        if half == 0:
                            pe.wait_ge(v_ok, ST * b + ST)
                        for m in range(KT):
                            n = AT_C[half] + m
                            ms = slice(m * P, (m + 1) * P)
                            step(n, work[:, n % 2, :], [((vhi[:, k, ms], vlo[:, k, ms]), (pthi[:, k, :], ptlo[:, k, :]))
                                                        for k in range(ST)])

                    def output(half):
                        pe.wait_ge(work_free, cnth(STEPS * b + (AT_C[half] + KT - 1)))
                        for t in range(TPC):
                            n = AT_C[half] + KT + t
                            ts = slice(t * P, (t + 1) * P)
                            step(n, work[:, n % 2, 0:D], [((chi[:, k, ts], clo[:, k, ts]), (ohi[:, k, :], olo[:, k, :]))
                                                          for k in range(KT)])

                    in_order(scores, turn, context, output)

            @block.scalar
            def _(act):
                act.sem_inc(exp_ok, CREDIT)
                act.wait_ge(loaded, 16 * len(loads))
                with act.Fori(0, B) as b:
                    for n, (w, m, c) in enumerate(QK):
                        act.wait_ge(work_full, STEPS * b + (STEPS + n + 1))
                        act.activation(qkhi[:, w, m, c * CH:(c + 1) * CH], work[:, n % 2, :], ACT.Identity,
                                       bias=bias[:, w * KT + m:w * KT + m + 1]).then_inc(cut_hi, 1)
                    for t in range(ST):
                        act.wait_ge(vf_ok, ST * b + (t + 1))
                        act.activation(vhi[:, t, :], vf[:, t % 2, :], ACT.Copy).then_inc(cut_hi, 1)

                    def context(half):
                        for m in range(KT):
                            n = AT_C[half] + m
                            act.wait_ge(work_full, STEPS * b + (STEPS + n + 1))
                            act.activation(chi[:, m, :], work[:, n % 2, :], ACT.Copy).then_inc(cut_hi, 1)

                    def scores(t):
                        g = ST * b + t
                        act.wait_ge(max_ok, nth(g))
                        act.wait_ge(turn_full, two_back(g))
                        act.activation(pr[:, t % 2, :], sc[:, t % 2, :], ACT.Exp, bias=neg[:, t % 2, 1:2], scale=scale,
                                       accum_out=sums[:, t // TPC, t % TPC:t % TPC + 1]).then_inc(exp_ok, 1)

                    def turn(t):
                        act.wait_ge(turn_full, cnth(ST * b + t))
                        if t == TPC:
                            act.wait_ge(work_full, STEPS * b + (STEPS + AT_C[0] + KT))
                        cs = slice(t % TPC * P, (t % TPC + 1) * P)
                        act.activation(pthi[:, :, cs], turned[:, :, :], ACT.Copy).then_inc(pt_hi, 1)

                    in_order(scores, turn, context, lambda half: None, turn_first=True)

            @block.vector
            def _(dve):
                dve.sem_inc(work_free, CREDIT)
                dve.sem_inc(pt_lo, 1)
                dve.sem_inc(turn_full, CREDIT)
                dve.wait_ge(loaded, 16 * len(loads))
                for t in range(NT):
                    ins = dve.tensor_tensor(X[:, t, :], X[:, t, :], ob[:, :], ALU.add)
                ins.then_inc(based, 1)
                dve.wait_ge(based, 1)
                with dve.Fori(0, B) as b:
                    count = [0]

                    def chain(ins):
                        ins.then_inc(own, 1)
                        count[0] += 1
                        dve.wait_ge(own, OWN * b + count[0])

                    for n, (w, m, c) in enumerate(QK):
                        hi, lo = (t[:, w, m, c * CH:(c + 1) * CH] for t in (qkhi, qklo))
                        dve.wait_ge(cut_hi, HIS * b + (n + 1))
                        dve.scalar_tensor_tensor(out=lo, in0=work[:, n % 2, :], scalar=bias[:, w * KT + m:w * KT + m + 1],
                                                 in1=f(hi), op0=ALU.add, op1=ALU.subtract).then_inc(work_free, 1)

                    def value_lo(t):
                        dve.wait_ge(cut_hi, HIS * b + (AT_V + t + 1))
                        dve.tensor_tensor(vlo[:, t, :], vf[:, t % 2, :], f(vhi[:, t, :]), ALU.subtract).then_inc(v_ok, 1)

                    for t in range(ST):
                        n = AT_V + t
                        dve.wait_ge(work_full, STEPS * b + (STEPS + n + 1))
                        if t >= 2:
                            dve.wait_ge(v_ok, ST * b + (t - 1))
                        dve.tensor_tensor(vf[:, t % 2, :], work[:, n % 2, 0:D], vb[:, :], ALU.add).then_inc(vf_ok, 1)
                        dve.wait_ge(vf_ok, ST * b + (t + 1))
                        dve.sem_inc(work_free, 1)
                        if t >= 1:
                            value_lo(t - 1)
                    value_lo(ST - 1)

                    def scores(t):
                        dve.wait_ge(sc_full, ST * b + (t + 1))
                        chain(dve.tensor_reduce(neg[:, t % 2, 0:1], sc[:, t % 2, :], AX.X, ALU.max, negate=True))
                        dve.tensor_scalar(neg[:, t % 2, 1:2], neg[:, t % 2, 0:1], scale, None, ALU.mult).then_inc(max_ok, 1)

                    def turn(t):
                        dve.wait_ge(pt_hi, ST * b + (t + 1))
                        cs = slice(t % TPC * P, (t % TPC + 1) * P)
                        dve.tensor_tensor(ptlo[:, :, cs], turned[:, :, :], f(pthi[:, :, cs]),
                                          ALU.subtract).then_inc(pt_lo, 1)

                    def context(half):
                        for m in range(KT):
                            n = AT_C[half] + m
                            dve.wait_ge(cut_hi, HIS * b + (AT_CH[half] + m + 1))
                            dve.tensor_tensor(clo[:, m, :], work[:, n % 2, :], f(chi[:, m, :]),
                                              ALU.subtract).then_inc(work_free, 1)
                        dve.wait_ge(exp_ok, cnth(ST * b + (TPC * (half + 1) - 1)))
                        chain(dve.reciprocal(inv[:, half, :], sums[:, half, :]))

                    def output(half):
                        for t in range(TPC):
                            n = AT_C[half] + KT + t
                            dve.wait_ge(work_full, STEPS * b + (STEPS + n + 1))
                            x = X[:, bass.ds(ST * b + half * TPC + t, 1), :].rearrange("p o d -> p (o d)")
                            dve.scalar_tensor_tensor(out=x, in0=work[:, n % 2, 0:D], scalar=inv[:, half, t:t + 1],
                                                     in1=x, op0=ALU.mult, op1=ALU.add).then_inc(work_free, 1)

                    in_order(scores, turn, context, output)
                    assert count[0] == OWN


def store(nc, X, out):
    with Phase(nc, "store") as ph:
        stored = ph.sem("stored")
        with nc.Block() as block:
            @block.sync
            def _(sp):
                sp.dma_start(out.rearrange("b (n p) d -> p (b n) d", p=P), X[:, :, :]).then_inc(stored, 16)
                sp.wait_ge(stored, 16)


def build(nc, i, out):
    def scratch(name, shape):
        return nc.dram_tensor(name, shape, F32, kind="Internal").ap()

    with ExitStack() as ctx:
        def sb(name, shape, dt=F32):
            return ctx.enter_context(nc.sbuf_tensor(name, shape, dt))

        X = sb("X", [P, NT, D])
        ident = sb("ident", [P, P])
        masks = sb("mask_qk", [P, P]), sb("mask_kq", [P, P])
        q16, k16 = scratch("q16", [2, 8, 4, 16, S]), scratch("k16", [2, 8, 4, 16, S])
        q8, k8 = scratch("q8", [2, 16, 4, 8, S]), scratch("k8", [2, 16, 1, 8, S])
        down = scratch("down", [8, 1, P, D])

        def channels(name):
            stack = ExitStack()
            return stack, [stack.enter_context(nc.sbuf_tensor(f"{name}_x{n}", [P, KT, T], F32R)) for n in ("hi", "lo")]

        def heads(name, norm, pieces, gains, project, dh, q, k, scale, causal, w_out, b_out):
            with ExitStack() as phases:
                first = [phases.enter_context(nc.sbuf_tensor(f"{name}_{n}0", [P, heads, S], F32R))
                         for n, heads in (("Q", 4), ("K", k.shape[2]))]
                V = phases.enter_context(nc.sbuf_tensor(f"{name}_V", [P, q.shape[1], ST, k.shape[2] * dh], F32))
                with ExitStack() as short:
                    out_weight = Weight(nc, phases, short, f"{name}_wo", [(0, D, w_out)])
                    stack, xn = channels(name)
                    short.enter_context(stack)
                    weight = Weight(nc, stack, stack, f"{name}_w", pieces, gains)
                    norm(xn, [weight, out_weight])
                    project(xn, weight, first, V)
                O = phases.enter_context(nc.sbuf_tensor(f"{name}_O", [P, ST, q.shape[1], 4 * dh], F32))
                attention(nc, f"{name}_at", first, q, k, V, O, ident, masks, dh, scale, causal)
                out_projection(nc, f"{name}_out", X, O, ident, out_weight, b_out)

        def ffn(name, w1, w2, rest, gate_w=None):
            stack, xn = channels(name)
            with stack:
                experts = Experts(nc, stack, f"{name}_e", w1, w2, gate_w)
                normed(nc, f"{name}_n", X, ident, xn, experts=experts)
                gated_ffn(nc, name, X, xn, ident, experts, rest)

        def layer0():
            yield lambda: heads(
                "a0", lambda xn, ws: normed(nc, "a0_n", X, ident, xn, RMS_EPS, weights=ws),
                [(0, D, i["L0_attn_a_Wq"]), (D, 3 * D, i["L0_attn_a_Wkv"])],
                (i["cols_L0_attn_a_g_q"], i["cols_L0_attn_a_g_kv"]),
                lambda xn, w, first, V: qkv(nc, "a0_p", xn, w, first, 16, q16, k16, P, V, D, q_bias=i["cols_L0_attn_a_bq"],
                                     k_bias=i["cols_L0_attn_a_bkv"], v_bias=i["L0_attn_a_bkv"][D:2 * D],
                                     head_gain=i["head_gain"]),
                16, q16, k16, 16 ** -0.5, False, i["L0_attn_a_Wo"], i["L0_attn_a_bo"])
            yield lambda: ffn("m0", i["moe_w1"], i["moe_w2"], True, i["moe_gate"])

            def wide():
                stack, xn = channels("b0")
                with stack:
                    weight = Weight(nc, stack, stack, "b0_w", [(0, 3 * D, i["wide_qkv"])])
                    out_weight = Weight(nc, stack, stack, "b0_wo", [(0, D, i["wide_out"])])
                    normed(nc, "b0_n", X, ident, xn, weights=[weight, out_weight])
                    wide_attention(nc, "b0", X, xn, ident, weight, i["cols_L0_attn_b_b_qkv"],
                                   i["L0_attn_b_b_qkv"][2 * D:3 * D], out_weight, i["L0_attn_b_b_out"])
            yield wide
            yield lambda: ffn("m1", i["moe_w1"], i["moe_w2"], True, i["moe_gate"])

        def layer1():
            yield lambda: heads(
                "a1", lambda xn, ws: normed(nc, "a1_n", X, ident, xn, LN_EPS, i["cols_L1_attn_a_ln_g"],
                                            i["cols_L1_attn_a_ln_b"], weights=ws),
                [(n * D, (n + 1) * D, i[f"L1_attn_a_W{w}"]) for n, w in enumerate("qkv")], None,
                lambda xn, w, first, V: qkv(nc, "a1_p", xn, w, first, 16, q16, k16, P, V, D, q_bias=i["cols_L1_attn_a_bq"],
                                     k_bias=i["cols_L1_attn_a_bk"], v_bias=i["L1_attn_a_bv"]),
                16, q16, k16, 16 ** -0.5, True, i["L1_attn_a_Wo"], i["L1_attn_a_bo"])
            yield lambda: ffn("f0", i["ffn_w1"], down, False)
            yield lambda: heads(
                "b1", lambda xn, ws: normed(nc, "b1_n", X, ident, xn, weights=ws),
                [(0, D, i["L1_attn_b_Wq"]), (D, D + 64, i["L1_attn_b_Wk"]), (D + 64, D + 128, i["L1_attn_b_Wv"])],
                None, lambda xn, w, first, V: qkv(nc, "b1_p", xn, w, first, 8, q8, k8, 64, V, 64),
                8, q8, k8, 8 ** -0.5, True, i["L1_attn_b_Wo"], None)
            yield lambda: ffn("f1", i["ffn_w1"], down, False)

        setup(nc, ident, masks)
        hadamard_down(nc, "had", ident, i["ffn_w2"], down, i["L0_attn_a_x"], X)
        for phase in [*layer0(), *layer1()]:
            phase()
        store(nc, X, out)


_DIRECT = ["L0_attn_a_x", "L0_attn_a_Wq", "L0_attn_a_Wkv", "L0_attn_a_bkv", "L0_attn_a_Wo",
           "L0_attn_a_bo", "L0_attn_b_b_qkv", "L0_attn_b_b_out", "L1_attn_a_Wq", "L1_attn_a_Wk", "L1_attn_a_Wv",
           "L1_attn_a_bv", "L1_attn_a_Wo", "L1_attn_a_bo", "L1_attn_b_Wq", "L1_attn_b_Wk", "L1_attn_b_Wv",
           "L1_attn_b_Wo"]


_COLUMNS = ["L0_attn_a_g_q", "L0_attn_a_g_kv", "L0_attn_a_bq", "L0_attn_a_bkv", "L0_attn_b_b_qkv",
            "L1_attn_a_ln_g", "L1_attn_a_ln_b", "L1_attn_a_bq", "L1_attn_a_bk"]


def lay_out(inputs):
    import numpy as np

    a = {n: np.asarray(v) for n, v in inputs.items()}
    out = {n: a[n] for n in _DIRECT}
    out |= {f"cols_{n}": a[n].reshape(-1, 128).T for n in _COLUMNS}
    out["head_gain"] = np.tile(a["L0_attn_a_g_head"], 128 // a["L0_attn_a_g_head"].size)[:, None]
    w1, w2 = a["L0_ffn_w1"], a["L0_ffn_w2"]
    E, D_, I2 = w1.shape
    I = I2 // 2
    moe1 = np.zeros((E + 1, D_, 3 * 128 - 16), w1.dtype)
    moe2 = np.zeros((E + 1, 2, 128, D_), w1.dtype)
    for e in range(E + 1):
        g, u = (w1[e, :, :I], w1[e, :, I:]) if e < E else (a["L0_ffn_sw1"].T, a["L0_ffn_sw2"].T)
        d = w2[e] if e < E else a["L0_ffn_sw3"].T
        moe1[e, :, 0:128], moe1[e, :, 128:256] = g[:, :128], u[:, :128]
        moe1[e, :, 256:256 + I - 128], moe1[e, :, 320:320 + I - 128] = g[:, 128:], u[:, 128:]
        moe2[e, 0], moe2[e, 1, :I - 128] = d[:128], d[128:]
    out["moe_w1"], out["moe_w2"], out["moe_gate"] = moe1, moe2, a["L0_ffn_gate_w"].T
    out["wide_qkv"], out["wide_out"] = a["L0_attn_b_w_qkv"].T, a["L0_attn_b_w_out"].T
    W1, W3 = a["L1_ffn_W1"].T, a["L1_ffn_W3"].T
    blocks = [np.concatenate([W1[:, n:n + 128], W3[:, n:n + 128]], axis=1) for n in range(0, W1.shape[1], 128)]
    out["ffn_w1"], out["ffn_w2"] = np.stack(blocks), a["L1_ffn_W2"].T
    return {n: np.ascontiguousarray(v) for n, v in out.items()}


def kernel(**inputs):
    import concourse.bacc as bacc
    from concourse.bass_utils import run_bass_kernel_spmd

    nc = bacc.Bacc("TRN2", target_bir_lowering=False, num_devices=1)
    arrays = {f"in_{n}": v for n, v in lay_out(inputs).items()}
    aps = {n[3:]: nc.dram_tensor(n, v.shape, mybir.dt.from_np(v.dtype), kind="ExternalInput").ap()
           for n, v in arrays.items()}
    out = nc.dram_tensor("out", inputs["L0_attn_a_x"].shape, F32, kind="ExternalOutput").ap()
    build(nc, aps, out)
    r = run_bass_kernel_spmd(nc, [arrays], core_ids=[0])
    return r.results[0]["out"]
```
